# Optimizing a Trainium2 kernel written in Bass

```python
import numpy as np
import jax
import jax.numpy as jnp

def _softmax(x, axis=-1):
    return jax.nn.softmax(x, axis=axis)

def _gelu(x):
    return jax.nn.gelu(x, approximate=True)

def _silu(x):
    return jax.nn.silu(x)

def _sigmoid(x):
    return jax.nn.sigmoid(x)

def _layernorm(x, axis=-1, eps=1e-05):
    m = jnp.mean(x, axis=axis, keepdims=True)
    v = jnp.var(x, axis=axis, keepdims=True)
    return (x - m) / jnp.sqrt(v + eps)

def _scatter_add(tgt, idx, src, axis=0):
    return tgt.at[idx].add(src)

def _segment_sum(src, seg, n):
    return jax.ops.segment_sum(src, seg, n)
kernel_name = 'mk_perceiver_d1_seqx_r8_8704a6'

def setup_inputs(seed: int=0):
    np.random.seed(seed)
    _w = jnp.asarray

    def _rec_inputs():
        import jax
        import jax.numpy as jnp
        _rk = jax.random.key(seed)
        x = -0.0003929 + 0.9999 * jax.random.normal(jax.random.fold_in(_rk, 1), (1, 64, 256), jnp.float32)
        _lenS = 64 - jax.random.randint(jax.random.fold_in(_rk, 7), (1,), 0, max(1, 64 // 4) + 1, jnp.int32)
        _lenS2 = 6272 - jax.random.randint(jax.random.fold_in(_rk, 8), (1,), 0, max(1, 6272 // 4) + 1, jnp.int32)
        _ctx_2048P = jax.random.normal(jax.random.fold_in(_rk, 11), (1, 16, 256), jnp.float32)
        _ctx_2048c = jax.random.dirichlet(jax.random.fold_in(_rk, 511), 0.3 * jnp.ones((16,), jnp.float32), (1, 6272))
        _ctx_2048t = jnp.einsum('bsk,bkd->bsd', _ctx_2048c, _ctx_2048P)
        _ctx_2048t = _ctx_2048t * jax.lax.rsqrt(jnp.mean(jnp.square(_ctx_2048t)) + 1e-12) * 0.953939
        ctx_2048 = -0.000514642 + 1.00011 * (_ctx_2048t + 0.3 * jax.random.normal(jax.random.fold_in(_rk, 611), (1, 6272, 256), jnp.float32))
        return (x, ctx_2048)
    x, ctx_2048 = _rec_inputs()

    def _L0_xattn_setup():
        import jax, jax.numpy as jnp
        import numpy as np
        DIM = 256
        NHEADS = 32
        HEAD_DIM = DIM // NHEADS
        EPS = 1e-06

        def _rmsnorm(t):
            return t * jax.lax.rsqrt(jnp.mean(t * t, axis=-1, keepdims=True) + EPS)
        key = jax.random.key(seed)
        kx, kc, kq, kk, kv = jax.random.split(key, 5)
        x = jax.random.normal(kx, (2, 512, DIM), dtype=jnp.float32)
        context = jax.random.normal(kc, (2, 64, DIM), dtype=jnp.float32)
        std = 0.02
        Wq = jax.random.normal(kq, (DIM, DIM), dtype=jnp.float32) * std
        Wk = jax.random.normal(kk, (DIM, DIM), dtype=jnp.float32) * std
        Wv = jax.random.normal(kv, (DIM, DIM), dtype=jnp.float32) * std
        return {'x': x, 'context': context, 'Wq': Wq, 'Wk': Wk, 'Wv': Wv}
    _L0_xattn_all = _L0_xattn_setup()
    _L0_xattn_in = {k: v for k, v in _L0_xattn_all.items() if k in ('Wq', 'Wk', 'Wv')}
    del _L0_xattn_all

    def _L0_attn_setup():
        import jax, jax.numpy as jnp
        import numpy as np
        BLOCK = 32
        NUM_HEADS = 16
        HEAD_DIM = 128
        FP4_GRID = jnp.array([0.0, 0.5, 1.0, 1.5, 2.0, 3.0, 4.0, 6.0], dtype=jnp.float32)

        def quantize_to_mxfp4(w, block_size=BLOCK):
            D, F = w.shape
            blocks = w.reshape(D // block_size, block_size, F)
            amax = jnp.max(jnp.abs(blocks), axis=1)
            e = jnp.floor(jnp.log2(jnp.maximum(amax, 1e-12) / 6.0))
            scale = jnp.exp2(e)
            v = blocks / scale[:, None, :]
            idx = jnp.argmin(jnp.abs(jnp.abs(v)[..., None] - FP4_GRID), axis=-1)
            codes = jnp.sign(v) * FP4_GRID[idx]
            return (codes.reshape(D, F).astype(jnp.float32), scale.astype(jnp.float32))

        def _mxfp4_matmul(x, codes, scales, block_size=BLOCK):
            w = codes * jnp.repeat(scales, block_size, axis=0)
            return x @ w
        key = jax.random.key(seed)
        ks = jax.random.split(key, 9)
        B, S, D = (2, 256, 256)
        feat = NUM_HEADS * HEAD_DIM
        x = jax.random.normal(ks[0], (B, S, D), dtype=jnp.float32)

        def make_w(k, din, dout):
            w = jax.random.normal(k, (din, dout), dtype=jnp.float32) * (1.0 / np.sqrt(din))
            return quantize_to_mxfp4(w, BLOCK)
        wq_codes, wq_scales = make_w(ks[1], D, feat)
        wk_codes, wk_scales = make_w(ks[2], D, feat)
        wv_codes, wv_scales = make_w(ks[3], D, feat)
        wo_codes, wo_scales = make_w(ks[4], feat, D)
        bq = jnp.zeros((feat,), jnp.float32)
        bk = jnp.zeros((feat,), jnp.float32)
        bv = jnp.zeros((feat,), jnp.float32)
        bo = jnp.zeros((D,), jnp.float32)
        return {'x': x, 'wq_codes': wq_codes, 'wq_scales': wq_scales, 'bq': bq, 'wk_codes': wk_codes, 'wk_scales': wk_scales, 'bk': bk, 'wv_codes': wv_codes, 'wv_scales': wv_scales, 'bv': bv, 'wo_codes': wo_codes, 'wo_scales': wo_scales, 'bo': bo}
    _L0_attn_all = _L0_attn_setup()
    _L0_attn_in = {k: v for k, v in _L0_attn_all.items() if k in ('wq_codes', 'wq_scales', 'bq', 'wk_codes', 'wk_scales', 'bk', 'wv_codes', 'wv_scales', 'bv', 'wo_codes', 'wo_scales', 'bo')}
    del _L0_attn_all

    def _L0_ffn_setup():
        import jax, jax.numpy as jnp
        import numpy as np
        TOPK = 2
        N_EXPERTS = 8
        ROUTE_SCALE = 1.0
        key = jax.random.key(seed)
        ks = jax.random.split(key, 7)
        B, T, C = (4, 256, 256)
        H = 176
        HS = 352
        E = N_EXPERTS
        s = 0.02
        return {'x': jax.random.normal(ks[0], (B, T, C), jnp.float32), 'gate_w': jax.random.normal(ks[1], (E, C), jnp.float32) * s, 'gate_bias': jnp.zeros((E,), jnp.float32), 'shared_gw': jax.random.normal(ks[2], (2 * HS, C), jnp.float32) * s, 'shared_dw': jax.random.normal(ks[3], (C, HS), jnp.float32) * s, 'up_w': jax.random.normal(ks[4], (E, 2 * H, C), jnp.float32) * s, 'down_w': jax.random.normal(ks[5], (E, C, H), jnp.float32) * s}
    _L0_ffn_all = _L0_ffn_setup()
    _L0_ffn_in = {k: v for k, v in _L0_ffn_all.items() if k in ('gate_w', 'gate_bias', 'shared_gw', 'shared_dw', 'up_w', 'down_w')}
    del _L0_ffn_all
    return {'x': x, 'ctx_2048': ctx_2048, 'L0_xattn_Wq': _L0_xattn_in['Wq'], 'L0_xattn_Wk': _L0_xattn_in['Wk'], 'L0_xattn_Wv': _L0_xattn_in['Wv'], 'L0_attn_wq_codes': _L0_attn_in['wq_codes'], 'L0_attn_wq_scales': _L0_attn_in['wq_scales'], 'L0_attn_bq': _L0_attn_in['bq'], 'L0_attn_wk_codes': _L0_attn_in['wk_codes'], 'L0_attn_wk_scales': _L0_attn_in['wk_scales'], 'L0_attn_bk': _L0_attn_in['bk'], 'L0_attn_wv_codes': _L0_attn_in['wv_codes'], 'L0_attn_wv_scales': _L0_attn_in['wv_scales'], 'L0_attn_bv': _L0_attn_in['bv'], 'L0_attn_wo_codes': _L0_attn_in['wo_codes'], 'L0_attn_wo_scales': _L0_attn_in['wo_scales'], 'L0_attn_bo': _L0_attn_in['bo'], 'L0_ffn_gate_w': _L0_ffn_in['gate_w'], 'L0_ffn_gate_bias': _L0_ffn_in['gate_bias'], 'L0_ffn_shared_gw': _L0_ffn_in['shared_gw'], 'L0_ffn_shared_dw': _L0_ffn_in['shared_dw'], 'L0_ffn_up_w': _L0_ffn_in['up_w'], 'L0_ffn_down_w': _L0_ffn_in['down_w']}

def reference(x, ctx_2048, L0_xattn_Wq, L0_xattn_Wk, L0_xattn_Wv, L0_attn_wq_codes, L0_attn_wq_scales, L0_attn_bq, L0_attn_wk_codes, L0_attn_wk_scales, L0_attn_bk, L0_attn_wv_codes, L0_attn_wv_scales, L0_attn_bv, L0_attn_wo_codes, L0_attn_wo_scales, L0_attn_bo, L0_ffn_gate_w, L0_ffn_gate_bias, L0_ffn_shared_gw, L0_ffn_shared_dw, L0_ffn_up_w, L0_ffn_down_w):
    import jax
    import jax.numpy as jnp

    def _L0_xattn_ref(x, context, Wq, Wk, Wv):
        import jax, jax.numpy as jnp
        import numpy as np
        DIM = 256
        NHEADS = 32
        HEAD_DIM = DIM // NHEADS
        EPS = 1e-06

        def _rmsnorm(t):
            return t * jax.lax.rsqrt(jnp.mean(t * t, axis=-1, keepdims=True) + EPS)
        b, n, _ = x.shape
        m = context.shape[1]
        q = x @ Wq.T
        k_raw = context @ Wk.T
        v_raw = context @ Wv.T
        q = q.reshape(b, n, NHEADS, HEAD_DIM).transpose(0, 2, 1, 3)
        kv = jnp.concatenate([k_raw, v_raw], axis=-1)
        kv = kv.reshape(b, m, NHEADS, HEAD_DIM, 2)
        k = kv[..., 0].transpose(0, 2, 1, 3)
        v = kv[..., 1].transpose(0, 2, 1, 3)
        q = _rmsnorm(q)
        k = _rmsnorm(k)
        scale = HEAD_DIM ** (-0.5)
        scores = jnp.einsum('bhnd,bhmd->bhnm', q, k) * scale
        attn = jax.nn.softmax(scores, axis=-1)
        out = jnp.einsum('bhnm,bhmd->bhnd', attn, v)
        return out.transpose(0, 2, 1, 3).reshape(b, n, NHEADS * HEAD_DIM)

    def _L0_attn_ref(x, wq_codes, wq_scales, bq, wk_codes, wk_scales, bk, wv_codes, wv_scales, bv, wo_codes, wo_scales, bo):
        import jax, jax.numpy as jnp
        import numpy as np
        BLOCK = 32
        NUM_HEADS = 16
        HEAD_DIM = 128
        FP4_GRID = jnp.array([0.0, 0.5, 1.0, 1.5, 2.0, 3.0, 4.0, 6.0], dtype=jnp.float32)

        def quantize_to_mxfp4(w, block_size=BLOCK):
            D, F = w.shape
            blocks = w.reshape(D // block_size, block_size, F)
            amax = jnp.max(jnp.abs(blocks), axis=1)
            e = jnp.floor(jnp.log2(jnp.maximum(amax, 1e-12) / 6.0))
            scale = jnp.exp2(e)
            v = blocks / scale[:, None, :]
            idx = jnp.argmin(jnp.abs(jnp.abs(v)[..., None] - FP4_GRID), axis=-1)
            codes = jnp.sign(v) * FP4_GRID[idx]
            return (codes.reshape(D, F).astype(jnp.float32), scale.astype(jnp.float32))

        def _mxfp4_matmul(x, codes, scales, block_size=BLOCK):
            w = codes * jnp.repeat(scales, block_size, axis=0)
            return x @ w
        B, S, D = x.shape
        q = _mxfp4_matmul(x, wq_codes, wq_scales) + bq
        k = _mxfp4_matmul(x, wk_codes, wk_scales) + bk
        v = _mxfp4_matmul(x, wv_codes, wv_scales) + bv
        q = q.reshape(B, S, NUM_HEADS, HEAD_DIM)
        k = k.reshape(B, S, NUM_HEADS, HEAD_DIM)
        v = v.reshape(B, S, NUM_HEADS, HEAD_DIM)
        scores = jnp.einsum('bqhd,bkhd->bhqk', q, k) / jnp.sqrt(jnp.float32(HEAD_DIM))
        attn = jax.nn.softmax(scores, axis=-1)
        out = jnp.einsum('bhqk,bkhd->bqhd', attn, v).reshape(B, S, NUM_HEADS * HEAD_DIM)
        return _mxfp4_matmul(out, wo_codes, wo_scales) + bo

    def _L0_ffn_ref(x, gate_w, gate_bias, shared_gw, shared_dw, up_w, down_w):
        import jax, jax.numpy as jnp
        import numpy as np
        TOPK = 2
        N_EXPERTS = 8
        ROUTE_SCALE = 1.0
        B, T, C = x.shape
        xf = x.reshape(-1, C)
        yg = xf @ shared_gw.T
        y, g = jnp.split(yg, 2, axis=-1)
        shared = jax.nn.silu(g) * y @ shared_dw.T
        scores = jax.nn.sigmoid(xf @ gate_w.T)
        _, topk_idx = jax.lax.top_k(scores + gate_bias, TOPK)
        w = jnp.take_along_axis(scores, topk_idx, axis=-1)
        w = w / jnp.sum(w, axis=-1, keepdims=True) * ROUTE_SCALE
        out = jnp.zeros_like(xf)
        for e in range(N_EXPERTS):
            we = jnp.sum(jnp.where(topk_idx == e, w, 0.0), axis=-1)
            gu = xf @ up_w[e].T
            g_e, u_e = jnp.split(gu, 2, axis=-1)
            h = jax.nn.silu(g_e) * u_e
            out = out + h @ down_w[e].T * we[:, None]
        return (shared + out).reshape(B, T, C)
    x = x + _L0_xattn_ref(_layernorm(x, axis=-1), ctx_2048, L0_xattn_Wq, L0_xattn_Wk, L0_xattn_Wv)
    x = x + _L0_attn_ref(_layernorm(x, axis=-1), L0_attn_wq_codes, L0_attn_wq_scales, L0_attn_bq, L0_attn_wk_codes, L0_attn_wk_scales, L0_attn_bk, L0_attn_wv_codes, L0_attn_wv_scales, L0_attn_bv, L0_attn_wo_codes, L0_attn_wo_scales, L0_attn_bo)
    x = x + _L0_ffn_ref(_layernorm(x, axis=-1), L0_ffn_gate_w, L0_ffn_gate_bias, L0_ffn_shared_gw, L0_ffn_shared_dw, L0_ffn_up_w, L0_ffn_down_w)
    return x

_drawn_inputs = setup_inputs


def setup_inputs(seed=0):
    import zlib

    import numpy as np

    out = dict(_drawn_inputs(seed))
    spreads = {'L0_attn_bq': (0.0, 0.68),
     'L0_attn_bk': (0.0, 0.8),
     'L0_attn_bv': (0.0, 0.1),
     'L0_attn_bo': (0.0, 0.1),
     'L0_ffn_gate_bias': (0.0, 0.8)}
    factors = {'L0_ffn_gate_w': 8.0,
     'L0_ffn_shared_gw': 2.971,
     'L0_ffn_shared_dw': 3.065,
     'L0_ffn_up_w': 6.077,
     'L0_ffn_down_w': 6.018}
    for name, (base, spread) in spreads.items():
        noise = np.random.default_rng([zlib.crc32(name.encode()), seed]).standard_normal(out[name].shape)
        drawn = base * np.exp(spread * noise) if base else spread * noise
        out[name] = jnp.asarray(drawn.astype(out[name].dtype))
    for name, factor in factors.items():
        out[name] = (out[name] * factor).astype(out[name].dtype)
    return out
```

```python
from contextlib import ExitStack

import concourse.bass as bass
from concourse import mybir

F32 = mybir.dt.float32
F32R = mybir.dt.float32r
F16 = mybir.dt.float16
BF16 = mybir.dt.bfloat16
U32 = mybir.dt.uint32
ACT = mybir.ActivationFunctionType
ALU = mybir.AluOpType
AX_X = mybir.AxisListType.X

P = 128
N = 64
D = 256
DC = D // P
M = 6272
T = M // P
XH, XD = 32, 8
PAIRS = XH // 2
HPC = 4
KC = XH // HPC
VW = 4 * XD + 1
HALF = N * XH // 2
SH, SD = 16, 128
FEAT = SH * SD
QB = 32
WS = 512
DEQ = 3
NSL = DC * FEAT // WS
E, TOPK, H, HS = 8, 2, 176, 352
HC = H // 2
U = 4
PROJ, KV, TR, PV = 3, 2, 1, -1
FIRST, LAST = -(PROJ + 1), T - PV
LOOP0 = 1 - PV
ITERS = (T - PROJ - 1 - LOOP0) // U
LOOP1 = LOOP0 + ITERS * U
LN_EPS, RMS_EPS = 1e-5, 1e-6


class Tile:

    def __init__(self, i, c):
        self.i, self.c = i, c

    def ahead(self, k):
        return Tile(self.i, self.c + k)

    def exists(self):
        return self.i is not None or 0 <= self.c < T

    def slot(self, n):
        return self.c % n

    def count(self, per=1, plus=0):
        at = per * self.c + plus
        if self.i is None:
            return at if at > 0 else None
        return self.i * (U * per) + at

    def number(self):
        return self.c if self.i is None else self.i * U + self.c


def steps(engine, body):
    for c in range(FIRST, LOOP0):
        body(Tile(None, c))
    with engine.Fori(0, ITERS) as i:
        for j in range(U):
            body(Tile(i, LOOP0 + j))
    for c in range(LOOP1, LAST + 1):
        body(Tile(None, c))


def wait(engine, semaphore, count):
    if count is not None:
        engine.wait_ge(semaphore, count)


def perceiver(nc, x, ctx_t, xwq, xwkv, codes, scales, qkv_bias, bo, gate_w, gate_bias,
              shared_gw, shared_dw, up_w, down_w, eye, expert_ids, out):
    with ExitStack() as stack:
        def sb(name, shape, dt=F32):
            return stack.enter_context(nc.sbuf_tensor(name, shape, dt))

        def sem(name):
            return stack.enter_context(nc.semaphore(name))

        once = {}

        def ready(name):
            if name not in once:
                once[name] = sem(name)
            return once[name]

        ident = sb("ident", [P, P])
        ident16 = sb("ident16", [P, P], F16)
        iota = sb("iota", [N, E])
        eps_ln = sb("eps_ln", [P, 1])
        eps_rms = sb("eps_rms", [P, 1])
        x_sb = sb("x_sb", [N, D])
        wq_sb = sb("wq_sb", [P, DC, D])
        wkv_f = sb("wkv_f", [P, DC, 2 * D])
        wkv_hi = sb("wkv_hi", [P, DC, 2 * D], F32R)
        wkv_lo = sb("wkv_lo", [P, DC, 2 * D], F32R)
        w_all = sb("w_all", [P, 4 * NSL, WS])
        s_ring = sb("s_ring", [P, DEQ, WS])
        bias_t = sb("bias_t", [SD, 3, SH])
        bo_sb = sb("bo_sb", [N, D])
        gate_sb = sb("gate_sb", [P, DC, E])
        gb_sb = sb("gb_sb", [N, E])
        sgw_sb = sb("sgw_sb", [P, DC, 2 * HS])
        sdw_sb = sb("sdw_sb", [P, 3, D])
        up_sb = sb("up_sb", [P, DC, E, 2 * H])
        dn_sb = sb("dn_sb", [HC, E, 2, D])
        ctx_f = sb("ctx_f", [P, 4, DC, P])
        ctx_hi = sb("ctx_hi", [P, 2, DC, P], F32R)
        ctx_lo = sb("ctx_lo", [P, 2, DC, P], F32R)
        kv_sb = sb("kv_sb", [P, 2, 2 * D])
        k_sq = sb("k_sq", [P, 2, D])
        k_ss = sb("k_ss", [P, 2, XH])
        k_ln = sb("k_ln", [P, 2, XH])
        k_r = sb("k_r", [P, 2, XH])
        k_n = sb("k_n", [P, 2, D])
        k12 = sb("k12", [P, 2, XH, 2, 2, XD], F16)
        v_sb = sb("v_sb", [P, 4, PAIRS, VW], F16)
        kT = sb("kT", [P, 2, KC, P], F16)
        q_blk = sb("q_blk", [P, KC, HPC, N], F16)
        zeros = sb("zeros", [P, PAIRS // 2 * VW], F16)
        room = sb("room", [P, 4 * HALF + 2 * HALF])
        probs = room[:, 0:4 * HALF].rearrange("p (s h n) -> p s h n", s=2, h=2)
        probs_lo = room[:, 4 * HALF:].bitcast(F16).rearrange("p (s h n) -> p s h n", s=2, h=2)
        tok = room[0:N, :].rearrange("p (w f) -> p w f", w=3)
        h_sb = sb("h_sb", [N, D])
        hT = sb("hT", [P, DC, N])
        bn = sb("bn", [N, 6])
        mv = sb("mv", [N, 2])
        rs = sb("rs", [N, 4])
        q_f = sb("q_f", [N, D])
        q_sq = sb("q_sq", [N, D])
        q_ss = sb("q_ss", [N, 3, XH])
        q_n = sb("q_n", [N, D])
        q_parts = sb("q_parts", [N, XH, 4, XD], F16)
        o_sb = sb("o_sb", [P, PAIRS, VW])
        o_sum = sb("o_sum", [P, PAIRS, 2 * XD])
        o_nrm = sb("o_nrm", [P, PAIRS, 2 * XD])
        o_den = sb("o_den", [P, PAIRS])
        o_cat = sb("o_cat", [N, PAIRS, 2, XD])
        x1 = sb("x1", [N, D])
        x1b = sb("x1b", [N, D])
        x2 = sb("x2", [N, D])
        qT = wkv_f[:].rearrange("p c (h n) -> p (c h) n", n=N)
        kTs = ctx_f[:].rearrange("p s c (h n) -> p (s c h) n", n=N)
        s_p = kv_sb[0:N].rearrange("p s (h n) -> p (s h) n", n=N)
        pT = q_blk[0:N].rearrange("p c h n -> p (c h n)").bitcast(F32).rearrange("p (h n) -> p h n", n=N)
        s_max = sb("s_max", [N, SH])
        s_sum = sb("s_sum", [N, SH])
        s_inv = sb("s_inv", [N, SH])
        g_sc = sb("g_sc", [N, E])
        g_sel = sb("g_sel", [N, E])
        g_top = sb("g_top", [N, E])
        g_idx = sb("g_idx", [N, E], U32)
        g_idf = sb("g_idf", [N, E])
        g_m1 = sb("g_m1", [N, E])
        g_m = sb("g_m", [N, E])
        g_w = sb("g_w", [N, E])
        g_sum = sb("g_sum", [N, 2])
        g_we = sb("g_we", [N, E])
        cuts = [0]
        for size in (2 * HS, 2 * HS, HS, E * H, 2 * E * N, 3 * N):
            cuts.append(cuts[-1] + size)
        sig, act_g, h_sh, h_ex, heT, hsT = (room[:, a:b] for a, b in zip(cuts, cuts[1:]))
        sig = sig[0:N].rearrange("p (s n) -> p s n", s=2)
        act_g = act_g[0:N].rearrange("p (s n) -> p s n", s=2)
        h_sh = h_sh[0:N]
        h_ex = h_ex[0:N].rearrange("p (e n) -> p e n", e=E)
        heT = heT[0:HC].rearrange("p (k n) -> p k n", n=N)
        hsT = hsT.rearrange("p (c n) -> p c n", n=N)

        ps = stack.enter_context(nc.psum_tensor("ps", [P, 8, 512], F32))
        ps_scores = [ps[:, 0:2, :], ps[:, 2:4, :]]
        ps_kv = ps[:, 4, :]
        ps_kT = ps[:, 5, :].bitcast(F16).rearrange("p (c m) -> p c m", c=KC)
        ps_o = [ps[:, 6 + b, 0:PAIRS // 2 * VW].rearrange("p (r v) -> p r v", v=VW) for b in range(2)]

        ctx_in = [sem(f"ctx_in{k}") for k in range(4)]
        ctx_hi_done, ctx_lo_done = sem("ctx_hi_done"), sem("ctx_lo_done")
        kv_mm, kv_copied, sq_done, ss_done = sem("kv_mm"), sem("kv_copied"), sem("sq_done"), sem("ss_done")
        ln_done, r_done, kn_done = sem("ln_done"), sem("r_done"), sem("kn_done")
        k1_done, k2_done, v1_done, v_done = sem("k1_done"), sem("k2_done"), sem("v1_done"), sem("v_done")
        kT_mm, kT_copied = sem("kT_mm"), sem("kT_copied")
        scores_mm, exp_done, lo_done, pv_done = sem("scores_mm"), sem("exp_done"), sem("lo_done"), sem("pv_done")
        slice_in = [sem(f"slice_in{k}") for k in range(DEQ)]
        deq_done = sem("deq_done")
        qkv_mm, qkv_out = sem("qkv_mm"), sem("qkv_out")
        up_mm, sig_done, gs_done, hid_done, hT_mm = (
            sem("up_mm"), sem("sig_done"), sem("gs_done"), sem("hid_done"), sem("hT_mm"))

        block = stack.enter_context(nc.Block())

        @block.sync
        def _(sp):
            sp.dma_start(x_sb[:], x).then_inc(ready("x_in"), 16)
            sp.dma_start(wkv_f[:], xwkv).then_inc(ready("wkv_in"), 16)

            def load(tile):
                wait(sp, ctx_hi_done, tile.count(plus=-3))
                wait(sp, ctx_lo_done, tile.count(plus=-3))
                sp.dma_start(ctx_f[:, tile.slot(4)], ctx_t[bass.ds(tile.number(), 1)].rearrange(
                    "t p c m -> p (t c) m")).then_inc(ctx_in[tile.slot(4)], 16)

            def load_slice(k, slot):
                sp.dma_start(w_all[:, bass.ds(k, 1)], codes[:, bass.ds(k, 1)]).then_inc(slice_in[slot], 16)
                src = scales[bass.ds(k, 1)].rearrange("a b n -> (a b) n")
                sp.dma_start(s_ring[:, slot], src.unsqueeze(1).to_broadcast([P // QB, QB, WS])).then_inc(
                    slice_in[slot], 16)

            ahead = U + LOOP0
            for t in range(2):
                load(Tile(None, t))
            sp.dma_start(wq_sb[:], xwq).then_inc(ready("wq_in"), 16)
            for t in range(2, ahead):
                load(Tile(None, t))
            for k in range(DEQ):
                load_slice(k, k)
            with sp.Fori(0, ITERS - 1) as i:
                for j in range(U):
                    load(Tile(i, ahead + j))
                for slot in range(DEQ):
                    sp.wait_ge(deq_done, i * DEQ + slot + 1)
                    load_slice(i * DEQ + (DEQ + slot), slot)
            for t in range(ahead + (ITERS - 1) * U, T):
                load(Tile(None, t))
            for k in range(DEQ * ITERS, 4 * NSL):
                sp.wait_ge(deq_done, k - DEQ + 1)
                load_slice(k, k % DEQ)
            for dst, src in ((bias_t[:], qkv_bias), (bo_sb[:], bo.to_broadcast([N, D])), (gate_sb[:], gate_w),
                             (gb_sb[:], gate_bias.to_broadcast([N, E])), (sgw_sb[:], shared_gw),
                             (sdw_sb[:, 0:2], shared_dw[0:2 * P].rearrange("(c p) n -> p c n", p=P)),
                             (sdw_sb[0:HS - 2 * P, 2], shared_dw[2 * P:HS]),
                             (up_sb[:], up_w), (dn_sb[:], down_w)):
                sp.dma_start(dst, src).then_inc(ready("tail_in"), 16)
            sp.wait_ge(ready("y"), 1)
            sp.dma_start(out, x1[:]).then_inc(ready("out_written"), 16)
            sp.wait_ge(ready("out_written"), 16)

        @block.gpsimd
        def _(pool):
            pool.memset(zeros[:], 0.0).then_inc(ready("zeros"), 1)
            pool.memset(q_blk[:], 0.0).then_inc(ready("q_blk_zeroed"), 1)
            pool.memset(v_sb[:, :, :, VW - 1], 1.0).then_inc(ready("v_ones"), 1)

            def multiply(k, slot, landed):
                pool.wait_ge(slice_in[slot], landed)
                w = w_all[:, bass.ds(k, 1), :].rearrange("p a n -> p (a n)")
                nc.gpsimd.tensor_tensor(w, w, s_ring[:, slot], ALU.mult).then_inc(deq_done, 1)

            def step(t):
                split, keys, kv = t.ahead(PROJ + 1), t.ahead(KV), t.ahead(PROJ)
                if split.exists():
                    wait(pool, ctx_hi_done, split.count(plus=1))
                    nc.gpsimd.tensor_tensor(ctx_lo[:, split.slot(2)], ctx_f[:, split.slot(4)],
                                            ctx_hi[:, split.slot(2)].bitcast(F32),
                                            ALU.subtract).then_inc(ctx_lo_done, 1)
                if keys.exists():
                    wait(pool, k1_done, keys.count(plus=1))
                    nc.gpsimd.tensor_tensor(
                        k12[:, keys.slot(2), :, :, 1, :],
                        k_n[:, keys.slot(2)].rearrange("p (h d) -> p h d", d=XD).unsqueeze(2)
                        .to_broadcast([P, XH, 2, XD]),
                        k12[:, keys.slot(2), :, :, 0, :], ALU.subtract).then_inc(k2_done, 1)
                if kv.exists():
                    wait(pool, kv_copied, kv.count(plus=1))
                    wait(pool, ss_done, kv.count(plus=-1))
                    nc.gpsimd.tensor_tensor(k_sq[:, kv.slot(2)], kv_sb[:, kv.slot(2), 0:D],
                                            kv_sb[:, kv.slot(2), 0:D], ALU.mult).then_inc(sq_done, 1)

            per = 2 * 16
            for c in range(FIRST, LOOP0):
                step(Tile(None, c))
            with pool.Fori(0, ITERS) as i:
                for j in range(U):
                    step(Tile(i, LOOP0 + j))
                    if j < DEQ:
                        multiply(i * DEQ + j, j, i * per + per)
            for c in range(LOOP1, LAST + 1):
                step(Tile(None, c))
            for k in range(DEQ * ITERS, 4 * NSL):
                multiply(k, k % DEQ, (k // DEQ + 1) * per)

        def layernorm_act(act, name):
            act.wait_ge(ready(name + "_stats"), 2)
            nc.scalar.activation(rs[:, 0:1], mv[:, 1:2], ACT.Ln, bias=eps_ln[0:N]).then_inc(ready(name + "_ln"), 1)
            act.wait_ge(ready(name + "_ln"), 1)
            nc.scalar.activation(rs[:, 1:2], rs[:, 0:1], ACT.Exp, scale=-0.5).then_inc(ready(name + "_r"), 1)

        @block.scalar
        def _(act):
            nc.scalar.preload_act_table_set("natural_log_exp_and_others")
            act.dma_start(ident[:], eye).then_inc(ready("eye_in"), 16)
            act.dma_start(iota[:], expert_ids).then_inc(ready("ids_in"), 16)
            act.wait_ge(ready("eps_set"), 2)
            layernorm_act(act, "ln1")
            act.wait_ge(ready("q_mm"), 1)
            nc.scalar.activation(q_f[:], ps[0:N, 4, 0:D], ACT.Copy).then_inc(ready("q_copied"), 1)
            act.wait_ge(ready("q_ss"), 1)
            nc.scalar.activation(q_ss[:, 1], q_ss[:, 0], ACT.Ln, bias=eps_rms[0:N],
                                 scale=1.0 / XD).then_inc(ready("q_ln"), 1)
            act.wait_ge(ready("q_ln"), 1)
            nc.scalar.activation(q_ss[:, 2], q_ss[:, 1], ACT.Exp, scale=-0.5).then_inc(ready("q_r"), 1)

            def exps(t, half):
                wait(act, scores_mm, t.count(2, half + 1))
                wait(act, pv_done, t.count(2, half - 3))
                nc.scalar.activation(probs[:, t.slot(2), half], ps_scores[half].rearrange("p b n -> p (b n)"),
                                     ACT.Exp).then_inc(exp_done, 1)

            def step(t):
                if t.exists():
                    exps(t, 0)
                r = t.ahead(KV)
                if r.exists():
                    a = r.slot(2)
                    wait(act, ss_done, r.count(plus=1))
                    nc.scalar.activation(k_ln[:, a], k_ss[:, a], ACT.Ln, bias=eps_rms[:],
                                         scale=1.0 / XD).then_inc(ln_done, 1)
                    wait(act, ln_done, r.count(plus=1))
                    wait(act, kn_done, r.count(plus=-1))
                    nc.scalar.activation(k_r[:, a], k_ln[:, a], ACT.Exp, scale=-0.5).then_inc(r_done, 1)
                if t.exists():
                    exps(t, 1)
                tr = t.ahead(TR)
                if tr.exists():
                    wait(act, kT_mm, tr.count(plus=1))
                    wait(act, scores_mm, tr.count(2, -2))
                    nc.scalar.activation(kT[:, tr.slot(2)], ps_kT, ACT.Copy).then_inc(kT_copied, 1)
                kv = t.ahead(PROJ)
                if kv.exists():
                    wait(act, kv_mm, kv.count(plus=1))
                    wait(act, sq_done, kv.count(plus=-1))
                    wait(act, v_done, kv.count(plus=-1))
                    wait(act, kn_done, kv.count(plus=-1))
                    nc.scalar.activation(kv_sb[:, kv.slot(2)], ps_kv, ACT.Copy).then_inc(kv_copied, 1)

            steps(act, step)

            layernorm_act(act, "ln2")
            act.wait_ge(ready("s_shifted"), 1)
            nc.scalar.activation(s_p, s_p, ACT.Exp, scale=float(SD) ** -0.5).then_inc(ready("s_exp"), 1)
            layernorm_act(act, "ln3")
            act.wait_ge(ready("gate_mm"), 1)
            nc.scalar.activation(g_sc[:], ps[0:N, 6, 0:E], ACT.Sigmoid).then_inc(ready("gate_scores"), 1)
            for g in range(E + 1):
                act.wait_ge(up_mm, g + 1)
                if g >= 2:
                    act.wait_ge(gs_done, g - 1)
                w = HS if g == 0 else H
                nc.scalar.activation(sig[:, g % 2, 0:w], ps[0:N, 1 if g == 0 else 2 + (g - 1) % 4, 0:w],
                                     ACT.Sigmoid).then_inc(sig_done, 1)

        def layernorm_dve(dve, name, src):
            st = ready(name + "_stats")
            nc.vector.bn_stats(bn[:], src).then_inc(st, 1)
            dve.wait_ge(st, 1)
            nc.vector.bn_aggr(mv[:], bn[:]).then_inc(st, 1)
            dve.wait_ge(st, 2)
            newton = ready(name + "_newton")
            nc.vector.tensor_scalar(rs[:, 2:3], mv[:, 1:2], LN_EPS, None, ALU.add).then_inc(newton, 1)
            dve.wait_ge(newton, 1)
            dve.wait_ge(ready(name + "_r"), 1)
            nc.vector.tensor_scalar(rs[:, 3:4], rs[:, 2:3], rs[:, 1:2], rs[:, 1:2], ALU.mult,
                                    ALU.mult).then_inc(newton, 1)
            dve.wait_ge(newton, 2)
            nc.vector.tensor_scalar(rs[:, 2:3], rs[:, 3:4], -0.5, 1.5, ALU.mult, ALU.add).then_inc(newton, 1)
            dve.wait_ge(newton, 3)
            nc.vector.tensor_scalar(rs[:, 3:4], rs[:, 2:3], rs[:, 1:2], None, ALU.mult).then_inc(newton, 1)
            dve.wait_ge(newton, 4)
            nc.vector.tensor_scalar(h_sb[:], src, mv[:, 0:1], rs[:, 3:4], ALU.subtract,
                                    ALU.mult).then_inc(ready(name + "_h"), 1)

        @block.vector
        def _(dve):
            nc.vector.memset(eps_ln[:], LN_EPS).then_inc(ready("eps_set"), 1)
            nc.vector.memset(eps_rms[:], RMS_EPS).then_inc(ready("eps_set"), 1)
            dve.wait_ge(ready("x_in"), 16)
            layernorm_dve(dve, "ln1", x_sb[:])
            dve.wait_ge(ready("eye_in"), 16)
            nc.vector.tensor_copy(ident16[:], ident[:]).then_inc(ready("ident16"), 1)
            dve.wait_ge(ready("wkv_in"), 16)
            nc.vector.tensor_copy(wkv_hi[:], wkv_f[:]).then_inc(ready("wkv_hi"), 1)
            dve.wait_ge(ready("wkv_hi"), 1)
            nc.vector.tensor_tensor(wkv_lo[:], wkv_f[:], wkv_hi[:].bitcast(F32), ALU.subtract).then_inc(
                ready("wkv_lo"), 1)
            dve.wait_ge(ready("ln1_hT_mm"), 1)
            nc.vector.tensor_copy(hT[:], ps[:, 5, 0:DC * N].rearrange("p (c n) -> p c n", c=DC)).then_inc(
                ready("ln1_hT"), 1)

            dve.wait_ge(ready("q_copied"), 1)
            nc.vector.tensor_tensor(q_sq[:], q_f[:], q_f[:], ALU.mult).then_inc(ready("q_sq"), 1)
            dve.wait_ge(ready("q_sq"), 1)
            nc.vector.tensor_reduce(q_ss[:, 0], q_sq[:].rearrange("p (h d) -> p h d", d=XD), AX_X,
                                    ALU.add).then_inc(ready("q_ss"), 1)
            dve.wait_ge(ready("q_r"), 1)
            nc.vector.scalar_tensor_tensor(
                q_n[:].rearrange("p (h d) -> p h d", d=XD), q_f[:].rearrange("p (h d) -> p h d", d=XD),
                float(XD) ** -0.5, q_ss[:, 2].unsqueeze(2).to_broadcast([N, XH, XD]),
                ALU.mult, ALU.mult).then_inc(ready("q_n"), 1)
            dve.wait_ge(ready("q_n"), 1)
            qn = q_n[:].rearrange("p (h d) -> p h d", d=XD)
            nc.vector.tensor_copy(q_parts[:, :, 0, :], qn).then_inc(ready("q_parts"), 1)
            nc.vector.tensor_copy(q_parts[:, :, 1, :], qn).then_inc(ready("q_parts"), 1)
            dve.wait_ge(ready("q_parts"), 2)
            for a in (2, 3):
                nc.vector.tensor_tensor(q_parts[:, :, a, :], qn, q_parts[:, :, 0, :], ALU.subtract).then_inc(
                    ready("q_parts"), 1)
            dve.wait_ge(ready("qT_mm"), 1)
            dve.wait_ge(ready("q_blk_zeroed"), 1)
            q_t = ps[:, 5, :].bitcast(F16)[:, 0:KC * N].rearrange("p (c n) -> p c n", c=KC)
            for h in range(HPC):
                rows = slice(h * 4 * XD, (h + 1) * 4 * XD)
                nc.vector.tensor_copy(q_blk[rows, :, h, :], q_t[rows]).then_inc(ready("q_blk"), 1)

            def low(t, half):
                a = probs[:, t.slot(2), half]
                wait(dve, exp_done, t.count(2, half + 1))
                wait(dve, pv_done, t.count(2, half - 3))
                nc.vector.tensor_tensor(probs_lo[:, t.slot(2), half], a, a.bitcast(BF16)[:, 1::2],
                                        ALU.subtract).then_inc(lo_done, 1)

            def step(t):
                split = t.ahead(PROJ + 1)
                if split.exists():
                    a = split.slot(4)
                    n = (split.c // 4 + 1) * 16
                    dve.wait_ge(ctx_in[a], n if split.i is None else split.i * (16 * U // 4) + n)
                    wait(dve, kv_mm, split.count(plus=-1))
                    nc.vector.tensor_copy(ctx_hi[:, split.slot(2)], ctx_f[:, a]).then_inc(ctx_hi_done, 1)
                r = t.ahead(KV)
                if r.exists():
                    v = kv_sb[:, r.slot(2), D:2 * D].rearrange("p (r v) -> p r v", v=2 * XD)
                    hi, lo = v_sb[:, r.slot(4), :, 0:2 * XD], v_sb[:, r.slot(4), :, 2 * XD:4 * XD]
                    wait(dve, kv_copied, r.count(plus=1))
                    wait(dve, pv_done, r.count(2, -6))
                    nc.vector.tensor_copy(hi, v).then_inc(v1_done, 1)
                    wait(dve, v1_done, r.count(plus=1))
                    nc.vector.tensor_tensor(lo, v, hi, ALU.subtract).then_inc(v_done, 1)
                    wait(dve, sq_done, r.count(plus=1))
                    wait(dve, ln_done, r.count(plus=-1))
                    nc.vector.tensor_reduce(k_ss[:, r.slot(2)], k_sq[:, r.slot(2)].rearrange(
                        "p (h d) -> p h d", d=XD), AX_X, ALU.add).then_inc(ss_done, 1)
                if t.exists():
                    low(t, 0)
                if r.exists():
                    kn = k_n[:, r.slot(2)].rearrange("p (h d) -> p h d", d=XD)
                    wait(dve, r_done, r.count(plus=1))
                    wait(dve, k2_done, r.count(plus=-1))
                    nc.vector.tensor_tensor(
                        kn, kv_sb[:, r.slot(2), 0:D].rearrange("p (h d) -> p h d", d=XD),
                        k_r[:, r.slot(2)].unsqueeze(2).to_broadcast([P, XH, XD]), ALU.mult).then_inc(kn_done, 1)
                    wait(dve, kn_done, r.count(plus=1))
                    wait(dve, kT_mm, r.count(plus=-1))
                    nc.vector.tensor_copy(k12[:, r.slot(2), :, :, 0, :], kn.unsqueeze(2).to_broadcast(
                        [P, XH, 2, XD])).then_inc(k1_done, 1)
                if t.exists():
                    low(t, 1)

            steps(dve, step)

            dve.wait_ge(pv_done, 2 * T)
            for b in range(2):
                nc.vector.tensor_copy(o_sb[:, b * PAIRS // 2:(b + 1) * PAIRS // 2], ps_o[b]).then_inc(ready("o_sb"), 1)
            dve.wait_ge(ready("o_sb"), 2)
            nc.vector.tensor_tensor(o_sum[:], o_sb[:, :, 0:2 * XD], o_sb[:, :, 2 * XD:4 * XD], ALU.add).then_inc(
                ready("o_sum"), 1)
            nc.vector.reciprocal(o_den[:], o_sb[:, :, VW - 1]).then_inc(ready("o_sum"), 1)
            dve.wait_ge(ready("o_sum"), 2)
            nc.vector.tensor_tensor(o_nrm[:], o_sum[:], o_den[:].unsqueeze(2).to_broadcast([P, PAIRS, 2 * XD]),
                                    ALU.mult).then_inc(ready("o_nrm"), 1)
            dve.wait_ge(ready("o_nrm"), 1)
            for h in range(2):
                nc.vector.tensor_copy(o_cat[:, :, h, :], o_nrm[h * N:(h + 1) * N, :, h * XD:(h + 1) * XD]).then_inc(
                    ready("o_cat"), 1)
            dve.wait_ge(ready("o_cat"), 2)
            nc.vector.tensor_tensor(x1[:], x_sb[:], o_cat[:].rearrange("p r h d -> p (r h d)"), ALU.add).then_inc(
                ready("x1"), 1)
            dve.wait_ge(ready("x1"), 1)
            layernorm_dve(dve, "ln2", x1[:])
            dve.wait_ge(ready("tail_in"), 9 * 16)
            nc.vector.tensor_tensor(x1b[:], x1[:], bo_sb[:], ALU.add).then_inc(ready("x1b"), 1)
            dve.wait_ge(ready("ln2_hT_mm"), 1)
            nc.vector.tensor_copy(hT[:], ps[:, 5, 0:DC * N].rearrange("p (c n) -> p c n", c=DC)).then_inc(
                ready("ln2_hT"), 1)
            for w in range(3):
                for b in range(FEAT // 512):
                    n = w * FEAT // 512 + b
                    dve.wait_ge(qkv_mm, n + 1)
                    nc.vector.tensor_copy(tok[:, w, b * 512:(b + 1) * 512], ps[0:N, n % 4]).then_inc(qkv_out, 1)
                if w:
                    dst, bank = ((qT, 4), (kTs, 6))[w - 1]
                    dve.wait_ge(ready(f"t{w}_mm"), 1)
                    nc.vector.tensor_tensor(
                        dst, ps[:, bank:bank + 2].rearrange("p b (h n) -> p (b h) n", n=N),
                        bias_t[:, w - 1].unsqueeze(2).to_broadcast([SD, SH, N]), ALU.add).then_inc(
                        ready("qkT"), 1)
            sc = ps[0:N, 0:2].rearrange("p b (h n) -> p (b h) n", n=N)
            dve.wait_ge(ready("s_mm"), 1)
            nc.vector.tensor_reduce(s_max[:], sc, AX_X, ALU.max).then_inc(ready("s_max"), 1)
            dve.wait_ge(ready("s_max"), 1)
            nc.vector.tensor_tensor(s_p, sc, s_max[:].unsqueeze(2).to_broadcast([N, SH, N]),
                                    ALU.subtract).then_inc(ready("s_shifted"), 1)
            dve.wait_ge(ready("s_exp"), 1)
            nc.vector.tensor_reduce(s_sum[:], s_p, AX_X, ALU.add).then_inc(ready("s_sum"), 1)
            dve.wait_ge(ready("s_sum"), 1)
            nc.vector.reciprocal(s_inv[:], s_sum[:]).then_inc(ready("s_inv"), 1)
            dve.wait_ge(ready("s_inv"), 1)
            nc.vector.tensor_tensor(s_p, s_p, s_inv[:].unsqueeze(2).to_broadcast([N, SH, N]),
                                    ALU.mult).then_inc(ready("s_p"), 1)
            dve.wait_ge(ready("pT_mm"), 1)
            nc.vector.tensor_copy(pT, ps[0:N, 2:4].rearrange("p b (h n) -> p (b h) n", n=N)).then_inc(
                ready("pT"), 1)
            dve.wait_ge(ready("oT_mm"), 1)
            nc.vector.tensor_tensor(
                qT, ps[:, 4:6].rearrange("p b (h n) -> p (b h) n", n=N),
                bias_t[:, 2].unsqueeze(2).to_broadcast([SD, SH, N]), ALU.add).then_inc(ready("oT"), 1)
            dve.wait_ge(ready("wo_mm"), 1)
            dve.wait_ge(ready("x1b"), 1)
            nc.vector.tensor_tensor(x2[:], ps[0:N, 6, 0:D], x1b[:], ALU.add).then_inc(ready("x2"), 1)
            dve.wait_ge(ready("x2"), 1)
            layernorm_dve(dve, "ln3", x2[:])
            dve.wait_ge(ready("ln3_hT_mm"), 1)
            nc.vector.tensor_copy(hT[:], ps[:, 5, 0:DC * N].rearrange("p (c n) -> p c n", c=DC)).then_inc(
                ready("ln3_hT"), 1)
            r = ready("route")
            route = [0]

            def link(i):
                route[0] += 1
                i.then_inc(r, 1)
                dve.wait_ge(r, route[0])

            dve.wait_ge(ready("gate_scores"), 1)
            dve.wait_ge(ready("ids_in"), 16)
            link(nc.vector.tensor_tensor(g_sel[:], g_sc[:], gb_sb[:], ALU.add))
            link(nc.vector.max(g_top[:], g_sel[:]))
            link(nc.vector.max_index(g_idx[:], g_top[:], g_sel[:]))
            link(nc.vector.tensor_copy(g_idf[:], g_idx[:]))
            link(nc.vector.tensor_scalar(g_m1[:], iota[:], g_idf[:, 0:1], None, ALU.is_equal))
            link(nc.vector.scalar_tensor_tensor(g_m[:], iota[:], g_idf[:, 1:2], g_m1[:], ALU.is_equal, ALU.add))
            link(nc.vector.tensor_tensor(g_w[:], g_m[:], g_sc[:], ALU.mult))
            link(nc.vector.tensor_reduce(g_sum[:, 0:1], g_w[:], AX_X, ALU.add))
            link(nc.vector.reciprocal(g_sum[:, 1:2], g_sum[:, 0:1]))
            link(nc.vector.tensor_scalar(g_we[:], g_w[:], g_sum[:, 1:2], None, ALU.mult))
            for g in range(E + 1):
                w = HS if g == 0 else H
                gate = ps[0:N, 1 if g == 0 else 2 + (g - 1) % 4, 0:w]
                up = ps[0:N, 0, 0:HS] if g == 0 else ps[0:N, 2 + (g - 1) % 4, H:2 * H]
                dve.wait_ge(sig_done, g + 1)
                nc.vector.tensor_tensor(act_g[:, g % 2, 0:w], gate, sig[:, g % 2, 0:w], ALU.mult).then_inc(gs_done, 1)
                dve.wait_ge(gs_done, g + 1)
                if g == 0:
                    nc.vector.tensor_tensor(h_sh, up, act_g[:, 0], ALU.mult).then_inc(hid_done, 1)
                else:
                    nc.vector.scalar_tensor_tensor(h_ex[:, g - 1], up, g_we[:, g - 1:g], act_g[:, g % 2, 0:w],
                                                   ALU.mult, ALU.mult).then_inc(hid_done, 1)
            dve.wait_ge(hT_mm, 1)
            nc.vector.tensor_copy(hsT[:, 0:2], ps[:, 0, 0:2 * N].rearrange("p (c n) -> p c n", n=N)).then_inc(
                ready("hsT"), 1)
            nc.vector.tensor_copy(hsT[0:HS - 2 * P, 2], ps[0:HS - 2 * P, 0, 2 * N:3 * N]).then_inc(ready("hsT"), 1)
            for b in range(2):
                dve.wait_ge(hT_mm, b + 2)
                nc.vector.tensor_copy(heT[:, b * E:(b + 1) * E], ps[0:HC, 6 + b].rearrange(
                    "p (c n) -> p c n", n=N)).then_inc(ready("heT"), 1)
            dve.wait_ge(ready("down_mm"), 1)
            nc.vector.tensor_tensor(x1[:], ps[0:N, 1, 0:D], x2[:], ALU.add).then_inc(ready("y"), 1)

        @block.tensor
        def _(pe):
            def transpose_h(name):
                pe.wait_ge(ready(name + "_h"), 1)
                for c in range(DC):
                    last = nc.tensor.transpose(ps[:, 5, c * N:(c + 1) * N], h_sb[:, c * P:(c + 1) * P],
                                               ident[0:N, 0:N])
                last.then_inc(ready(name + "_hT_mm"), 1)
                pe.wait_ge(ready(name + "_hT"), 1)

            def contract(dst, rhs, **flags):
                for c in range(DC):
                    last = nc.tensor.matmul(dst, hT[:, c, :], rhs(c), start=(c == 0), stop=(c == DC - 1))
                return last

            pe.wait_ge(ready("eye_in"), 16)
            transpose_h("ln1")
            pe.wait_ge(ready("wq_in"), 16)
            contract(ps[0:N, 4, 0:D], lambda c: wq_sb[:, c, :]).then_inc(ready("q_mm"), 1)
            pe.wait_ge(ready("zeros"), 1)
            for b in range(2):
                nc.tensor.matmul(ps[:, 6 + b, 0:PAIRS // 2 * VW], zeros[:, 0:P], zeros[:],
                                 start=True, stop=True, skip_group_check=True)
            pe.wait_ge(ready("ident16"), 1)
            pe.wait_ge(ready("q_parts"), 4)
            for c in range(KC):
                last = nc.tensor.transpose(
                    ps[:, 5, :].bitcast(F16)[:, c * N:(c + 1) * N],
                    q_parts[:, c * HPC:(c + 1) * HPC].rearrange("p h a d -> p (h a d)"), ident16[0:N, 0:N])
            last.then_inc(ready("qT_mm"), 1)
            pe.wait_ge(ready("q_blk"), HPC)
            pe.wait_ge(ready("wkv_lo"), 1)
            pe.wait_ge(ready("v_ones"), 1)

            def scores(t, half):
                if half == 0:
                    wait(pe, kT_copied, t.count(plus=1))
                wait(pe, exp_done, t.count(2, half - 1))
                for c in range(KC // 2):
                    last = nc.tensor.matmul(
                        ps_scores[half][:, c // 2, c % 2 * HPC * N:(c % 2 + 1) * HPC * N],
                        kT[:, t.slot(2), half * KC // 2 + c], q_blk[:, half * KC // 2 + c].rearrange(
                            "p h n -> p (h n)"), start=True, stop=True)
                last.then_inc(scores_mm, 1)

            def values(t, half):
                wait(pe, lo_done, t.count(2, half + 1))
                if half == 0:
                    wait(pe, v_done, t.count(plus=1))
                hi = probs[:, t.slot(2), half].bitcast(BF16)[:, 1::2]
                lo = probs_lo[:, t.slot(2), half]
                for r in range(PAIRS // 2):
                    for part in (hi, lo):
                        last = nc.tensor.matmul(ps_o[half][:, r], part[:, r * P:(r + 1) * P],
                                                v_sb[:, t.slot(4), half * PAIRS // 2 + r], start=False,
                                                stop=False, skip_group_check=True)
                last.then_inc(pv_done, 1)

            def step(t):
                pv, tr, kv = t.ahead(PV), t.ahead(TR), t.ahead(PROJ)
                for half in range(2):
                    if t.exists():
                        scores(t, half)
                    if pv.exists():
                        values(pv, half)
                if tr.exists():
                    wait(pe, k2_done, tr.count(plus=1))
                    wait(pe, kT_copied, tr.count())
                    for c in range(KC):
                        rows = k12[:, tr.slot(2), c * HPC:(c + 1) * HPC].rearrange("p h q a d -> p (h q a d)")
                        last = nc.tensor.transpose(ps_kT[:, c], rows, ident16[:])
                    last.then_inc(kT_mm, 1)
                if kv.exists():
                    wait(pe, ctx_lo_done, kv.count(plus=1))
                    wait(pe, kv_copied, kv.count())
                    a = kv.slot(2)
                    terms = [(lhs[:, a, c], rhs[:, c]) for c in range(DC)
                             for lhs, rhs in ((ctx_hi, wkv_hi), (ctx_hi, wkv_lo), (ctx_lo, wkv_hi))]
                    for n, (lhs, rhs) in enumerate(terms):
                        last = nc.tensor.matmul(ps_kv, lhs, rhs, start=(n == 0), stop=(n == len(terms) - 1))
                    last.then_inc(kv_mm, 1)

            steps(pe, step)

            transpose_h("ln2")
            for w in range(3):
                for b in range(FEAT // 512):
                    n = w * FEAT // 512 + b
                    if n >= 4:
                        pe.wait_ge(qkv_out, n - 3)
                    pe.wait_ge(deq_done, w * NSL + DC * FEAT // 512 - (FEAT // 512 - 1 - b))
                    contract(ps[0:N, n % 4], lambda c: w_all[:, w * NSL + c * FEAT // 512 + b]).then_inc(qkv_mm, 1)
                if w:
                    bank = (4, 6)[w - 1]
                    pe.wait_ge(qkv_out, w * FEAT // 512)
                    for h in range(SH):
                        last = nc.tensor.transpose(ps[:, bank + h // 8, h % 8 * N:(h % 8 + 1) * N],
                                                   tok[:, w - 1, h * SD:(h + 1) * SD], ident[0:N, 0:N])
                    last.then_inc(ready(f"t{w}_mm"), 1)
            pe.wait_ge(ready("qkT"), 2)
            pe.wait_ge(qkv_out, 3 * FEAT // 512)
            for h in range(SH):
                last = nc.tensor.matmul(ps[0:N, h // 8, h % 8 * N:(h % 8 + 1) * N], qT[:, h], kTs[:, h],
                                        start=True, stop=True)
            last.then_inc(ready("s_mm"), 1)
            pe.wait_ge(ready("s_p"), 1)
            for h in range(SH):
                last = nc.tensor.transpose(ps[0:N, 2 + h // 8, h % 8 * N:(h % 8 + 1) * N], s_p[:, h],
                                           ident[0:N, 0:N])
            last.then_inc(ready("pT_mm"), 1)
            pe.wait_ge(ready("pT"), 1)
            for h in range(SH):
                last = nc.tensor.matmul(ps[:, 4 + h // 8, h % 8 * N:(h % 8 + 1) * N],
                                        tok[:, 2, h * SD:(h + 1) * SD], pT[:, h], start=True, stop=True)
            last.then_inc(ready("oT_mm"), 1)
            pe.wait_ge(ready("oT"), 1)
            pe.wait_ge(deq_done, 4 * NSL)
            wo = w_all[:, 3 * NSL:].rearrange("p s (h n) -> p (s h) n", n=D)
            for h in range(SH):
                last = nc.tensor.matmul(ps[0:N, 6, 0:D], qT[:, h], wo[:, h], start=(h == 0), stop=(h == SH - 1))
            last.then_inc(ready("wo_mm"), 1)

            pe.wait_ge(ready("tail_in"), 9 * 16)
            transpose_h("ln3")
            contract(ps[0:N, 6, 0:E], lambda c: gate_sb[:, c, :]).then_inc(ready("gate_mm"), 1)
            contract(ps[0:N, 0, 0:HS], lambda c: sgw_sb[:, c, 0:HS])
            contract(ps[0:N, 1, 0:HS], lambda c: sgw_sb[:, c, HS:2 * HS]).then_inc(up_mm, 1)
            for e in range(E):
                if e >= 4:
                    pe.wait_ge(hid_done, e - 2)
                contract(ps[0:N, 2 + e % 4, 0:2 * H], lambda c: up_sb[:, c, e, :]).then_inc(up_mm, 1)
            pe.wait_ge(hid_done, 1)
            for c in range(3):
                w = min(P, HS - c * P)
                last = nc.tensor.transpose(ps[0:w, 0, c * N:(c + 1) * N], h_sh[:, c * P:c * P + w],
                                           ident[0:N, 0:N])
            last.then_inc(hT_mm, 1)
            pe.wait_ge(ready("gate_scores"), 1)
            for e in range(E):
                pe.wait_ge(hid_done, e + 2)
                for c in range(2):
                    k = 2 * e + c
                    last = nc.tensor.transpose(ps[0:HC, 6 + k // 8, k % 8 * N:(k % 8 + 1) * N],
                                               h_ex[:, e, c * HC:(c + 1) * HC], ident[0:N, 0:N])
                if e % 4 == 3:
                    last.then_inc(hT_mm, 1)
            pe.wait_ge(ready("hsT"), 2)
            for c in range(3):
                w = min(P, HS - c * P)
                nc.tensor.matmul(ps[0:N, 1, 0:D], hsT[0:w, c], sdw_sb[0:w, c], start=(c == 0), stop=False)
            for k in range(2 * E):
                if k % 8 == 0:
                    pe.wait_ge(ready("heT"), k // 8 + 1)
                last = nc.tensor.matmul(ps[0:N, 1, 0:D], heT[:, k], dn_sb[:, k // 2, k % 2], start=False,
                                        stop=(k == 2 * E - 1))
            last.then_inc(ready("down_mm"), 1)


def kernel(x, ctx_2048, L0_xattn_Wq, L0_xattn_Wk, L0_xattn_Wv, L0_attn_wq_codes, L0_attn_wq_scales,
           L0_attn_bq, L0_attn_wk_codes, L0_attn_wk_scales, L0_attn_bk, L0_attn_wv_codes,
           L0_attn_wv_scales, L0_attn_bv, L0_attn_wo_codes, L0_attn_wo_scales, L0_attn_bo,
           L0_ffn_gate_w, L0_ffn_gate_bias, L0_ffn_shared_gw, L0_ffn_shared_dw, L0_ffn_up_w,
           L0_ffn_down_w):
    import numpy as np
    import concourse.bacc as bacc
    from concourse.bass_utils import run_bass_kernel_spmd

    def rows(w):
        w = np.asarray(w)
        return w.reshape(DC, P, w.shape[1]).transpose(1, 0, 2)

    wkv = np.concatenate([np.asarray(L0_xattn_Wk), np.asarray(L0_xattn_Wv)])
    wkv = wkv.reshape(XH, XD, 2, D).transpose(2, 0, 1, 3).reshape(2 * D, D)
    codes = [rows(c).reshape(P, NSL, WS) for c in (L0_attn_wq_codes, L0_attn_wk_codes, L0_attn_wv_codes)]
    codes.append(np.asarray(L0_attn_wo_codes).reshape(SH, SD, D).transpose(1, 0, 2).reshape(P, NSL, WS))
    nb = P // QB
    scales = [np.asarray(c).reshape(DC, nb, FEAT // WS, WS).transpose(0, 2, 1, 3).reshape(NSL, nb, WS)
              for c in (L0_attn_wq_scales, L0_attn_wk_scales, L0_attn_wv_scales)]
    scales.append(np.asarray(L0_attn_wo_scales).reshape(NSL, WS // D, nb, D).transpose(0, 2, 1, 3)
                  .reshape(NSL, nb, WS))
    up = np.asarray(L0_ffn_up_w).reshape(E * 2 * H, D).T
    arrays = {
        "x": np.asarray(x).reshape(N, D),
        "ctx_t": np.asarray(ctx_2048).reshape(T, P, DC, P).transpose(0, 3, 2, 1),
        "xwq": rows(np.asarray(L0_xattn_Wq).T),
        "xwkv": rows(wkv.T),
        "codes": np.concatenate(codes, axis=1),
        "scales": np.concatenate(scales),
        "qkv_bias": np.stack([np.asarray(b).reshape(SH, SD) for b in (L0_attn_bq, L0_attn_bk, L0_attn_bv)])
        .transpose(2, 0, 1),
        "bo": np.asarray(L0_attn_bo).reshape(1, D),
        "gate_w": rows(np.asarray(L0_ffn_gate_w).T),
        "gate_bias": np.asarray(L0_ffn_gate_bias).reshape(1, E),
        "shared_gw": rows(np.asarray(L0_ffn_shared_gw).T),
        "shared_dw": np.asarray(L0_ffn_shared_dw).T,
        "up_w": rows(up).reshape(P, DC, E, 2 * H),
        "down_w": np.asarray(L0_ffn_down_w).transpose(2, 0, 1).reshape(2, HC, E, D).transpose(1, 2, 0, 3),
        "eye": np.eye(P, dtype=np.float32),
        "expert_ids": np.tile(np.arange(E, dtype=np.float32), (N, 1)),
    }
    arrays = {n: np.ascontiguousarray(a) for n, a in arrays.items()}
    nc = bacc.Bacc("TRN2", target_bir_lowering=False, num_devices=1)
    args = [nc.dram_tensor(n, a.shape, mybir.dt.from_np(a.dtype), kind="ExternalInput").ap()
            for n, a in arrays.items()]
    out = nc.dram_tensor("out", (N, D), F32, kind="ExternalOutput").ap()
    perceiver(nc, *args, out)
    result = run_bass_kernel_spmd(nc, [arrays], core_ids=[0])
    return result.results[0]["out"].reshape(1, N, D)
```

```python
from contextlib import ExitStack

import concourse.bass as bass
from concourse import mybir

F32 = mybir.dt.float32
F32R = mybir.dt.float32r
F16 = mybir.dt.float16
BF16 = mybir.dt.bfloat16
U32 = mybir.dt.uint32
ACT = mybir.ActivationFunctionType
ALU = mybir.AluOpType
AX_X = mybir.AxisListType.X

P = 128
N = 64
D = 256
DC = D // P
M = 6272
T = M // P
XH, XD = 32, 8
PAIRS = XH // 2
HPC = 4
KC = XH // HPC
VW = 4 * XD + 1
HALF = N * XH // 2
SH, SD = 16, 128
FEAT = SH * SD
QB = 32
WS = 1024
POOLED = 384
NSL = DC * FEAT // WS
NQKV = 3 * NSL
E, TOPK, H, HS = 8, 2, 176, 352
HC = H // 2
U = 4
PROJ, KV, TR, PV = 4, 3, 2, -1
FIRST, LAST = -(PROJ + 1), T - PV
LOOP0 = 1 - PV
ITERS = (T - PROJ - 1 - LOOP0) // U
LOOP1 = LOOP0 + ITERS * U
LN_EPS, RMS_EPS = 1e-5, 1e-6


class Tile:

    def __init__(self, i, c):
        self.i, self.c = i, c

    def ahead(self, k):
        return Tile(self.i, self.c + k)

    def exists(self):
        return self.i is not None or 0 <= self.c < T

    def slot(self, n):
        return self.c % n

    def count(self, per=1, plus=0):
        at = per * self.c + plus
        if self.i is None:
            return at if at > 0 else None
        return self.i * (U * per) + at

    def number(self):
        return self.c if self.i is None else self.i * U + self.c


def steps(engine, body):
    for c in range(FIRST, LOOP0):
        body(Tile(None, c))
    with engine.Fori(0, ITERS) as i:
        for j in range(U):
            body(Tile(i, LOOP0 + j))
    for c in range(LOOP1, LAST + 1):
        body(Tile(None, c))


def wait(engine, semaphore, count):
    if count is not None:
        engine.wait_ge(semaphore, count)


def perceiver(nc, x, ctx_t, xwq, xwkv, codes, scales, qkv_bias, bo, gate_w, gate_bias,
              shared_gw, shared_dw, up_w, down_w, eye, expert_ids, out):
    with ExitStack() as stack:
        def sb(name, shape, dt=F32):
            return stack.enter_context(nc.sbuf_tensor(name, shape, dt))

        def sem(name):
            return stack.enter_context(nc.semaphore(name))

        once = {}

        def ready(name):
            if name not in once:
                once[name] = sem(name)
            return once[name]

        ident = sb("ident", [P, P])
        ident16 = sb("ident16", [P, P], F16)
        iota = sb("iota", [N, E])
        eps_ln = sb("eps_ln", [P, 1])
        eps_rms = sb("eps_rms", [P, 1])
        x_sb = sb("x_sb", [N, D])
        wq_sb = sb("wq_sb", [P, DC, D])
        wkv_f = sb("wkv_f", [P, DC, 2 * D])
        wkv_hi = sb("wkv_hi", [P, DC, 2 * D], F32R)
        wkv_lo = sb("wkv_lo", [P, DC, 2 * D], F32R)
        w_all = sb("w_all", [P, 4 * NSL, WS])
        s_ring = sb("s_ring", [P, 2, WS])
        bias_t = sb("bias_t", [SD, 3, SH])
        bo_sb = sb("bo_sb", [N, D])
        gate_sb = sb("gate_sb", [P, DC, E])
        gb_sb = sb("gb_sb", [N, E])
        sgw_sb = sb("sgw_sb", [P, DC, 2 * HS])
        sdw_sb = sb("sdw_sb", [P, 3, D])
        up_sb = sb("up_sb", [P, DC, E, 2 * H])
        dn_sb = sb("dn_sb", [HC, E, 2, D])
        ctx_f = sb("ctx_f", [P, 4, DC, P])
        ctx_hi = sb("ctx_hi", [P, 2, DC, P], F32R)
        ctx_lo = sb("ctx_lo", [P, 2, DC, P], F32R)
        kv_sb = sb("kv_sb", [P, 2, 2 * D])
        k_sq = sb("k_sq", [P, 2, D])
        k_ss = sb("k_ss", [P, 2, XH])
        k_ln = sb("k_ln", [P, 2, XH])
        k_r = sb("k_r", [P, 2, XH])
        k_n = sb("k_n", [P, 2, D])
        k12 = sb("k12", [P, 2, XH, 2, 2, XD], F16)
        v_flat = sb("v_flat", [P, 4 * PAIRS * VW], F16)
        v_sb = v_flat[:].rearrange("p (s r v) -> p s r v", s=4, r=PAIRS)
        kT = sb("kT", [P, 2, KC, P], F16)
        q_blk = sb("q_blk", [P, KC, HPC, N], F16)
        zeros = sb("zeros", [P, PAIRS // 2 * VW], F16)
        room = sb("room", [P, 4 * HALF + 2 * HALF])
        probs = room[:, 0:4 * HALF].rearrange("p (s h n) -> p s h n", s=2, h=2)
        probs_lo = room[:, 4 * HALF:].bitcast(F16).rearrange("p (s h n) -> p s h n", s=2, h=2)
        tok = room[0:N, :].rearrange("p (w f) -> p w f", w=3)
        h_sb = sb("h_sb", [N, D])
        hT = sb("hT", [P, DC, N])
        bn = sb("bn", [N, 6])
        mv = sb("mv", [N, 2])
        rs = sb("rs", [N, 4])
        q_f = sb("q_f", [N, D])
        q_sq = sb("q_sq", [N, D])
        q_ss = sb("q_ss", [N, 3, XH])
        q_n = sb("q_n", [N, D])
        q_parts = sb("q_parts", [N, XH, 4, XD], F16)
        o_sb = sb("o_sb", [P, PAIRS, VW])
        o_sum = sb("o_sum", [P, PAIRS, 2 * XD])
        o_nrm = o_sum
        o_den = sb("o_den", [P, PAIRS])
        o_cat = sb("o_cat", [N, PAIRS, 2, XD])
        x1 = sb("x1", [N, D])
        x1b, x2 = q_f, q_sq
        qT = wkv_f[:].rearrange("p c (h n) -> p (c h) n", n=N)
        s_slots = [s_ring[:, 0], s_ring[:, 1],
                   v_flat[:, 0:2 * WS].bitcast(F32)]
        wo_s_slots = [kT[:].rearrange("p s c m -> p (s c m)").bitcast(F32),
                      k12[:].rearrange("p s h q a d -> p (s h q a d)").bitcast(F32)]
        kTs = ctx_f[:].rearrange("p s c (h n) -> p (s c h) n", n=N)
        s_p = kv_sb[0:N].rearrange("p s (h n) -> p (s h) n", n=N)
        pT = q_blk[0:N].rearrange("p c h n -> p (c h n)").bitcast(F32).rearrange("p (h n) -> p h n", n=N)
        s_max = sb("s_max", [N, SH])
        s_sum = sb("s_sum", [N, SH])
        s_inv = sb("s_inv", [N, SH])
        g_sc = sb("g_sc", [N, E])
        g_sel = sb("g_sel", [N, E])
        g_top = sb("g_top", [N, E])
        g_idx = sb("g_idx", [N, E], U32)
        g_idf = sb("g_idf", [N, E])
        g_m1 = sb("g_m1", [N, E])
        g_m = sb("g_m", [N, E])
        g_w = sb("g_w", [N, E])
        g_sum = sb("g_sum", [N, 2])
        g_we = sb("g_we", [N, E])
        cuts = [0]
        for size in (2 * HS, 2 * HS, HS, E * H, 2 * E * N, 3 * N):
            cuts.append(cuts[-1] + size)
        sig, act_g, h_sh, h_ex, heT, hsT = (room[:, a:b] for a, b in zip(cuts, cuts[1:]))
        sig = sig[0:N].rearrange("p (s n) -> p s n", s=2)
        act_g = act_g[0:N].rearrange("p (s n) -> p s n", s=2)
        h_sh = h_sh[0:N]
        h_ex = h_ex[0:N].rearrange("p (e n) -> p e n", e=E)
        heT = heT[0:HC].rearrange("p (k n) -> p k n", n=N)
        hsT = hsT.rearrange("p (c n) -> p c n", n=N)

        ps = stack.enter_context(nc.psum_tensor("ps", [P, 8, 512], F32))
        ps_scores = [ps[:, 0:2, :], ps[:, 2:4, :]]
        ps_kv = ps[:, 4, :]
        ps_kT = ps[:, 5, :].bitcast(F16).rearrange("p (c m) -> p c m", c=KC)
        ps_o = [ps[:, 6 + b, 0:PAIRS // 2 * VW].rearrange("p (r v) -> p r v", v=VW) for b in range(2)]

        ctx_in = [sem(f"ctx_in{k}") for k in range(4)]
        ctx_hi_done, ctx_lo_done = sem("ctx_hi_done"), sem("ctx_lo_done")
        kv_mm, kv_copied, sq_done, ss_done = sem("kv_mm"), sem("kv_copied"), sem("sq_done"), sem("ss_done")
        ln_done, r_done, kn_done = sem("ln_done"), sem("r_done"), sem("kn_done")
        k1_done, k2_done, v1_done, v_done = sem("k1_done"), sem("k2_done"), sem("v1_done"), sem("v_done")
        kT_mm, kT_copied = sem("kT_mm"), sem("kT_copied")
        scores_mm, exp_done, lo_done, pv_done = sem("scores_mm"), sem("exp_done"), sem("lo_done"), sem("pv_done")
        low_pooled = sem("low_pooled")
        scales_in = [sem(f"scales_in{k}") for k in range(3)]
        wo_scales_in = [sem(f"wo_scales_in{k}") for k in range(2)]
        deq_done, wo_deq_done = sem("deq_done"), sem("wo_deq_done")
        qkv_mm, qkv_out = sem("qkv_mm"), sem("qkv_out")
        up_mm, sig_done, gs_done, hid_done, hT_mm = (
            sem("up_mm"), sem("sig_done"), sem("gs_done"), sem("hid_done"), sem("hT_mm"))

        block = stack.enter_context(nc.Block())

        @block.sync
        def _(sp):
            sp.dma_start(x_sb[:], x).then_inc(ready("x_in"), 16)
            sp.dma_start(wkv_f[:], xwkv).then_inc(ready("wkv_in"), 16)

            def load(tile):
                wait(sp, ctx_hi_done, tile.count(plus=-3))
                wait(sp, ctx_lo_done, tile.count(plus=-3))
                sp.dma_start(ctx_f[:, tile.slot(4)], ctx_t[bass.ds(tile.number(), 1)].rearrange(
                    "t p c m -> p (t c) m")).then_inc(ctx_in[tile.slot(4)], 16)

            def load_codes(k, landed):
                sp.dma_start(w_all[:, bass.ds(k, 1)], codes[:, bass.ds(k, 1)]).then_inc(landed, 16)

            def load_scales(k, slot, landed):
                sp.dma_start(slot, scales[k].unsqueeze(1).to_broadcast([P // QB, QB, WS])).then_inc(landed, 16)

            ahead = U + LOOP0
            for t in range(2):
                load(Tile(None, t))
            sp.dma_start(wq_sb[:], xwq).then_inc(ready("wq_in"), 16)
            for t in range(2, ahead):
                load(Tile(None, t))
            turns = ITERS - 1
            assert turns <= NQKV
            with sp.Fori(0, turns) as i:
                for j in range(U):
                    load(Tile(i, ahead + j))
                load_codes(i, ready("codes_in"))
            for t in range(ahead + turns * U, T):
                load(Tile(None, t))
            for k in range(turns, NQKV):
                load_codes(k, ready("codes_in"))
            for n in range(2):
                load_scales(n, s_slots[n], scales_in[n])
            for k in range(NQKV, 4 * NSL):
                load_codes(k, ready("wo_codes_in"))
            for dst, src in ((bias_t[:], qkv_bias), (bo_sb[:], bo.to_broadcast([N, D])), (gate_sb[:], gate_w),
                             (gb_sb[:], gate_bias.to_broadcast([N, E])), (sgw_sb[:], shared_gw),
                             (sdw_sb[:, 0:2], shared_dw[0:2 * P].rearrange("(c p) n -> p c n", p=P)),
                             (sdw_sb[0:HS - 2 * P, 2], shared_dw[2 * P:HS]),
                             (up_sb[:], up_w), (dn_sb[:], down_w)):
                sp.dma_start(dst, src).then_inc(ready("tail_in"), 16)
            sp.wait_ge(pv_done, 2 * T)
            load_scales(2, s_slots[2], scales_in[2])
            for m in range(2):
                load_scales(NQKV + m, wo_s_slots[m], wo_scales_in[m])
            for n in range(3, NQKV):
                sp.wait_ge(deq_done, n - 2)
                load_scales(n, s_slots[n % 3], scales_in[n % 3])
                if n - 3 in range(2, NSL):
                    m = n - 3
                    sp.wait_ge(wo_deq_done, m - 1)
                    load_scales(NQKV + m, wo_s_slots[m % 2], wo_scales_in[m % 2])
            sp.wait_ge(ready("y"), 1)
            sp.dma_start(out, x1[:]).then_inc(ready("out_written"), 16)
            sp.wait_ge(ready("out_written"), 16)

        @block.gpsimd
        def _(pool):
            pool.memset(zeros[:], 0.0).then_inc(ready("zeros"), 1)
            pool.memset(q_blk[:], 0.0).then_inc(ready("q_blk_zeroed"), 1)
            pool.memset(v_sb[:, :, :, VW - 1], 1.0).then_inc(ready("v_ones"), 1)

            def step(t):
                split, keys, sq = t.ahead(PROJ + 1), t.ahead(TR), t.ahead(KV)
                if sq.exists():
                    wait(pool, kv_copied, sq.count(plus=1))
                    wait(pool, ss_done, sq.count(plus=-1))
                    nc.gpsimd.tensor_tensor(k_sq[:, sq.slot(2)], kv_sb[:, sq.slot(2), 0:D],
                                            kv_sb[:, sq.slot(2), 0:D], ALU.mult).then_inc(sq_done, 1)
                if keys.exists():
                    wait(pool, k1_done, keys.count(plus=1))
                    nc.gpsimd.tensor_tensor(
                        k12[:, keys.slot(2), :, :, 1, :],
                        k_n[:, keys.slot(2)].rearrange("p (h d) -> p h d", d=XD).unsqueeze(2)
                        .to_broadcast([P, XH, 2, XD]),
                        k12[:, keys.slot(2), :, :, 0, :], ALU.subtract).then_inc(k2_done, 1)
                if split.exists():
                    wait(pool, ctx_hi_done, split.count(plus=1))
                    nc.gpsimd.tensor_tensor(ctx_lo[:, split.slot(2)], ctx_f[:, split.slot(4)],
                                            ctx_hi[:, split.slot(2)].bitcast(F32),
                                            ALU.subtract).then_inc(ctx_lo_done, 1)
                if t.exists():
                    wait(pool, exp_done, t.count(2, 2))
                    wait(pool, pv_done, t.count(2, -2))
                    a = probs[:, t.slot(2), 1, HALF - POOLED:HALF]
                    nc.gpsimd.tensor_tensor(probs_lo[:, t.slot(2), 1, HALF - POOLED:HALF], a,
                                            a.bitcast(BF16)[:, 1::2], ALU.subtract).then_inc(low_pooled, 1)

            steps(pool, step)
            pool.wait_ge(ready("wo_codes_in"), NSL * 16)
            for m in range(NSL):
                pool.wait_ge(wo_scales_in[m % 2], (m // 2 + 1) * 16)
                w = w_all[:, NQKV + m]
                nc.gpsimd.tensor_tensor(w, w, wo_s_slots[m % 2], ALU.mult).then_inc(wo_deq_done, 1)

        def layernorm_act(act, name):
            act.wait_ge(ready(name + "_stats"), 2)
            nc.scalar.activation(rs[:, 0:1], mv[:, 1:2], ACT.Ln, bias=eps_ln[0:N]).then_inc(ready(name + "_ln"), 1)
            act.wait_ge(ready(name + "_ln"), 1)
            nc.scalar.activation(rs[:, 1:2], rs[:, 0:1], ACT.Exp, scale=-0.5).then_inc(ready(name + "_r"), 1)

        @block.scalar
        def _(act):
            nc.scalar.preload_act_table_set("natural_log_exp_and_others")
            act.dma_start(ident[:], eye).then_inc(ready("eye_in"), 16)
            act.dma_start(iota[:], expert_ids).then_inc(ready("ids_in"), 16)
            act.wait_ge(ready("eps_set"), 2)
            layernorm_act(act, "ln1")
            act.wait_ge(ready("q_mm"), 1)
            nc.scalar.activation(q_f[:], ps[0:N, 4, 0:D], ACT.Copy).then_inc(ready("q_copied"), 1)
            act.wait_ge(ready("q_ss"), 1)
            nc.scalar.activation(q_ss[:, 1], q_ss[:, 0], ACT.Ln, bias=eps_rms[0:N],
                                 scale=1.0 / XD).then_inc(ready("q_ln"), 1)
            act.wait_ge(ready("q_ln"), 1)
            nc.scalar.activation(q_ss[:, 2], q_ss[:, 1], ACT.Exp, scale=-0.5).then_inc(ready("q_r"), 1)

            def exps(t, half):
                wait(act, scores_mm, t.count(2, half + 1))
                wait(act, pv_done, t.count(2, half - 3))
                nc.scalar.activation(probs[:, t.slot(2), half], ps_scores[half].rearrange("p b n -> p (b n)"),
                                     ACT.Exp).then_inc(exp_done, 1)

            def step(t):
                if t.exists():
                    exps(t, 0)
                if t.exists():
                    exps(t, 1)
                r = t.ahead(KV)
                if r.exists():
                    a = r.slot(2)
                    wait(act, ss_done, r.count(plus=1))
                    nc.scalar.activation(k_ln[:, a], k_ss[:, a], ACT.Ln, bias=eps_rms[:],
                                         scale=1.0 / XD).then_inc(ln_done, 1)
                    wait(act, ln_done, r.count(plus=1))
                    wait(act, kn_done, r.count(plus=-1))
                    nc.scalar.activation(k_r[:, a], k_ln[:, a], ACT.Exp, scale=-0.5).then_inc(r_done, 1)
                kv = t.ahead(PROJ)
                if kv.exists():
                    wait(act, kv_mm, kv.count(plus=1))
                    wait(act, sq_done, kv.count(plus=-1))
                    wait(act, v_done, kv.count(plus=-1))
                    wait(act, kn_done, kv.count(plus=-1))
                    nc.scalar.activation(kv_sb[:, kv.slot(2)], ps_kv, ACT.Copy).then_inc(kv_copied, 1)
                tr = t.ahead(TR)
                if tr.exists():
                    wait(act, kT_mm, tr.count(plus=1))
                    wait(act, scores_mm, tr.count(2, -2))
                    nc.scalar.activation(kT[:, tr.slot(2)], ps_kT, ACT.Copy).then_inc(kT_copied, 1)

            steps(act, step)

            layernorm_act(act, "ln2")
            for n in range(NQKV):
                act.wait_ge(qkv_mm, n + 1)
                nc.scalar.activation(tok[:, n // NSL, n % NSL * 512:(n % NSL + 1) * 512], ps[0:N, n % 4],
                                     ACT.Copy).then_inc(qkv_out, 1)
            act.wait_ge(ready("s_shifted"), 1)
            nc.scalar.activation(s_p, s_p, ACT.Exp, scale=float(SD) ** -0.5).then_inc(ready("s_exp"), 1)
            layernorm_act(act, "ln3")
            act.wait_ge(ready("gate_mm"), 1)
            nc.scalar.activation(g_sc[:], ps[0:N, 6, 0:E], ACT.Sigmoid).then_inc(ready("gate_scores"), 1)
            for g in range(E + 1):
                act.wait_ge(up_mm, g + 1)
                if g >= 2:
                    act.wait_ge(gs_done, g - 1)
                w = HS if g == 0 else H
                nc.scalar.activation(sig[:, g % 2, 0:w], ps[0:N, 1 if g == 0 else 2 + (g - 1) % 4, 0:w],
                                     ACT.Sigmoid).then_inc(sig_done, 1)

        def layernorm_dve(dve, name, src):
            st = ready(name + "_stats")
            nc.vector.bn_stats(bn[:], src).then_inc(st, 1)
            dve.wait_ge(st, 1)
            nc.vector.bn_aggr(mv[:], bn[:]).then_inc(st, 1)
            dve.wait_ge(st, 2)
            newton = ready(name + "_newton")
            nc.vector.tensor_scalar(rs[:, 2:3], mv[:, 1:2], LN_EPS, None, ALU.add).then_inc(newton, 1)
            dve.wait_ge(newton, 1)
            dve.wait_ge(ready(name + "_r"), 1)
            nc.vector.tensor_scalar(rs[:, 3:4], rs[:, 2:3], rs[:, 1:2], rs[:, 1:2], ALU.mult,
                                    ALU.mult).then_inc(newton, 1)
            dve.wait_ge(newton, 2)
            nc.vector.tensor_scalar(rs[:, 2:3], rs[:, 3:4], -0.5, 1.5, ALU.mult, ALU.add).then_inc(newton, 1)
            dve.wait_ge(newton, 3)
            nc.vector.tensor_scalar(rs[:, 3:4], rs[:, 2:3], rs[:, 1:2], None, ALU.mult).then_inc(newton, 1)
            dve.wait_ge(newton, 4)
            nc.vector.tensor_scalar(h_sb[:], src, mv[:, 0:1], rs[:, 3:4], ALU.subtract,
                                    ALU.mult).then_inc(ready(name + "_h"), 1)

        @block.vector
        def _(dve):
            nc.vector.memset(eps_ln[:], LN_EPS).then_inc(ready("eps_set"), 1)
            nc.vector.memset(eps_rms[:], RMS_EPS).then_inc(ready("eps_set"), 1)
            dve.wait_ge(ready("x_in"), 16)
            layernorm_dve(dve, "ln1", x_sb[:])
            dve.wait_ge(ready("eye_in"), 16)
            nc.vector.tensor_copy(ident16[:], ident[:]).then_inc(ready("ident16"), 1)
            dve.wait_ge(ready("wkv_in"), 16)
            nc.vector.tensor_copy(wkv_hi[:], wkv_f[:]).then_inc(ready("wkv_hi"), 1)
            dve.wait_ge(ready("wkv_hi"), 1)
            nc.vector.tensor_tensor(wkv_lo[:], wkv_f[:], wkv_hi[:].bitcast(F32), ALU.subtract).then_inc(
                ready("wkv_lo"), 1)
            dve.wait_ge(ready("ln1_hT_mm"), 1)
            nc.vector.tensor_copy(hT[:], ps[:, 5, 0:DC * N].rearrange("p (c n) -> p c n", c=DC)).then_inc(
                ready("ln1_hT"), 1)

            dve.wait_ge(ready("q_copied"), 1)
            nc.vector.tensor_tensor(q_sq[:], q_f[:], q_f[:], ALU.mult).then_inc(ready("q_sq"), 1)
            dve.wait_ge(ready("q_sq"), 1)
            nc.vector.tensor_reduce(q_ss[:, 0], q_sq[:].rearrange("p (h d) -> p h d", d=XD), AX_X,
                                    ALU.add).then_inc(ready("q_ss"), 1)
            dve.wait_ge(ready("q_r"), 1)
            nc.vector.scalar_tensor_tensor(
                q_n[:].rearrange("p (h d) -> p h d", d=XD), q_f[:].rearrange("p (h d) -> p h d", d=XD),
                float(XD) ** -0.5, q_ss[:, 2].unsqueeze(2).to_broadcast([N, XH, XD]),
                ALU.mult, ALU.mult).then_inc(ready("q_n"), 1)
            dve.wait_ge(ready("q_n"), 1)
            qn = q_n[:].rearrange("p (h d) -> p h d", d=XD)
            nc.vector.tensor_copy(q_parts[:, :, 0, :], qn).then_inc(ready("q_parts"), 1)
            nc.vector.tensor_copy(q_parts[:, :, 1, :], qn).then_inc(ready("q_parts"), 1)
            dve.wait_ge(ready("q_parts"), 2)
            for a in (2, 3):
                nc.vector.tensor_tensor(q_parts[:, :, a, :], qn, q_parts[:, :, 0, :], ALU.subtract).then_inc(
                    ready("q_parts"), 1)
            dve.wait_ge(ready("qT_mm"), 1)
            dve.wait_ge(ready("q_blk_zeroed"), 1)
            q_t = ps[:, 5, :].bitcast(F16)[:, 0:KC * N].rearrange("p (c n) -> p c n", c=KC)
            for h in range(HPC):
                rows = slice(h * 4 * XD, (h + 1) * 4 * XD)
                nc.vector.tensor_copy(q_blk[rows, :, h, :], q_t[rows]).then_inc(ready("q_blk"), 1)

            def low(t, half):
                w = HALF - half * POOLED
                a = probs[:, t.slot(2), half, 0:w]
                wait(dve, exp_done, t.count(2, half + 1))
                wait(dve, pv_done, t.count(2, half - 3))
                nc.vector.tensor_tensor(probs_lo[:, t.slot(2), half, 0:w], a, a.bitcast(BF16)[:, 1::2],
                                        ALU.subtract).then_inc(lo_done, 1)

            def step(t):
                split = t.ahead(PROJ + 1)
                if split.exists():
                    a = split.slot(4)
                    n = (split.c // 4 + 1) * 16
                    dve.wait_ge(ctx_in[a], n if split.i is None else split.i * (16 * U // 4) + n)
                    wait(dve, kv_mm, split.count(plus=-1))
                    nc.vector.tensor_copy(ctx_hi[:, split.slot(2)], ctx_f[:, a]).then_inc(ctx_hi_done, 1)
                r = t.ahead(KV)
                if r.exists():
                    wait(dve, sq_done, r.count(plus=1))
                    wait(dve, ln_done, r.count(plus=-1))
                    nc.vector.tensor_reduce(k_ss[:, r.slot(2)], k_sq[:, r.slot(2)].rearrange(
                        "p (h d) -> p h d", d=XD), AX_X, ALU.add).then_inc(ss_done, 1)
                if t.exists():
                    low(t, 0)
                if r.exists():
                    v = kv_sb[:, r.slot(2), D:2 * D].rearrange("p (r v) -> p r v", v=2 * XD)
                    hi, lo = v_sb[:, r.slot(4), :, 0:2 * XD], v_sb[:, r.slot(4), :, 2 * XD:4 * XD]
                    wait(dve, kv_copied, r.count(plus=1))
                    wait(dve, pv_done, r.count(2, -6))
                    nc.vector.tensor_copy(hi, v).then_inc(v1_done, 1)
                    wait(dve, v1_done, r.count(plus=1))
                    nc.vector.tensor_tensor(lo, v, hi, ALU.subtract).then_inc(v_done, 1)
                if t.exists():
                    low(t, 1)
                if r.exists():
                    kn = k_n[:, r.slot(2)].rearrange("p (h d) -> p h d", d=XD)
                    wait(dve, r_done, r.count(plus=1))
                    wait(dve, k2_done, r.count(plus=-1))
                    nc.vector.tensor_tensor(
                        kn, kv_sb[:, r.slot(2), 0:D].rearrange("p (h d) -> p h d", d=XD),
                        k_r[:, r.slot(2)].unsqueeze(2).to_broadcast([P, XH, XD]), ALU.mult).then_inc(kn_done, 1)
                    wait(dve, kn_done, r.count(plus=1))
                    wait(dve, kT_mm, r.count(plus=-1))
                    nc.vector.tensor_copy(k12[:, r.slot(2), :, :, 0, :], kn.unsqueeze(2).to_broadcast(
                        [P, XH, 2, XD])).then_inc(k1_done, 1)

            steps(dve, step)

            dve.wait_ge(pv_done, 2 * T)
            for b in range(2):
                nc.vector.tensor_copy(o_sb[:, b * PAIRS // 2:(b + 1) * PAIRS // 2], ps_o[b]).then_inc(ready("o_sb"), 1)
            dve.wait_ge(ready("o_sb"), 2)
            nc.vector.tensor_tensor(o_sum[:], o_sb[:, :, 0:2 * XD], o_sb[:, :, 2 * XD:4 * XD], ALU.add).then_inc(
                ready("o_sum"), 1)
            nc.vector.reciprocal(o_den[:], o_sb[:, :, VW - 1]).then_inc(ready("o_sum"), 1)
            dve.wait_ge(ready("o_sum"), 2)
            nc.vector.tensor_tensor(o_nrm[:], o_sum[:], o_den[:].unsqueeze(2).to_broadcast([P, PAIRS, 2 * XD]),
                                    ALU.mult).then_inc(ready("o_nrm"), 1)
            dve.wait_ge(ready("o_nrm"), 1)
            for h in range(2):
                nc.vector.tensor_copy(o_cat[:, :, h, :], o_nrm[h * N:(h + 1) * N, :, h * XD:(h + 1) * XD]).then_inc(
                    ready("o_cat"), 1)
            dve.wait_ge(ready("o_cat"), 2)
            nc.vector.tensor_tensor(x1[:], x_sb[:], o_cat[:].rearrange("p r h d -> p (r h d)"), ALU.add).then_inc(
                ready("x1"), 1)
            dve.wait_ge(ready("x1"), 1)
            layernorm_dve(dve, "ln2", x1[:])
            dve.wait_ge(ready("tail_in"), 9 * 16)
            nc.vector.tensor_tensor(x1b[:], x1[:], bo_sb[:], ALU.add).then_inc(ready("x1b"), 1)
            dve.wait_ge(ready("ln2_hT_mm"), 1)
            nc.vector.tensor_copy(hT[:], ps[:, 5, 0:DC * N].rearrange("p (c n) -> p c n", c=DC)).then_inc(
                ready("ln2_hT"), 1)
            dve.wait_ge(ready("codes_in"), NQKV * 16)
            for w in range(3):
                for n in range(w * NSL, (w + 1) * NSL):
                    dve.wait_ge(scales_in[n % 3], (n // 3 + 1) * 16)
                    nc.vector.tensor_tensor(w_all[:, n], w_all[:, n], s_slots[n % 3], ALU.mult).then_inc(
                        deq_done, 1)
                if w:
                    dst, bank = ((qT, 4), (kTs, 6))[w - 1]
                    dve.wait_ge(ready(f"t{w}_mm"), 1)
                    nc.vector.tensor_tensor(
                        dst, ps[:, bank:bank + 2].rearrange("p b (h n) -> p (b h) n", n=N),
                        bias_t[:, w - 1].unsqueeze(2).to_broadcast([SD, SH, N]), ALU.add).then_inc(
                        ready("qkT"), 1)
            sc = ps[0:N, 0:2].rearrange("p b (h n) -> p (b h) n", n=N)
            dve.wait_ge(ready("s_mm"), 1)
            nc.vector.tensor_reduce(s_max[:], sc, AX_X, ALU.max).then_inc(ready("s_max"), 1)
            dve.wait_ge(ready("s_max"), 1)
            nc.vector.tensor_tensor(s_p, sc, s_max[:].unsqueeze(2).to_broadcast([N, SH, N]),
                                    ALU.subtract).then_inc(ready("s_shifted"), 1)
            dve.wait_ge(ready("s_exp"), 1)
            nc.vector.tensor_reduce(s_sum[:], s_p, AX_X, ALU.add).then_inc(ready("s_sum"), 1)
            dve.wait_ge(ready("s_sum"), 1)
            nc.vector.reciprocal(s_inv[:], s_sum[:]).then_inc(ready("s_inv"), 1)
            dve.wait_ge(ready("s_inv"), 1)
            nc.vector.tensor_tensor(s_p, s_p, s_inv[:].unsqueeze(2).to_broadcast([N, SH, N]),
                                    ALU.mult).then_inc(ready("s_p"), 1)
            dve.wait_ge(ready("pT_mm"), 1)
            nc.vector.tensor_copy(pT, ps[0:N, 2:4].rearrange("p b (h n) -> p (b h) n", n=N)).then_inc(
                ready("pT"), 1)
            dve.wait_ge(ready("oT_mm"), 1)
            nc.vector.tensor_tensor(
                qT, ps[:, 4:6].rearrange("p b (h n) -> p (b h) n", n=N),
                bias_t[:, 2].unsqueeze(2).to_broadcast([SD, SH, N]), ALU.add).then_inc(ready("oT"), 1)
            dve.wait_ge(ready("wo_mm"), 1)
            dve.wait_ge(ready("x1b"), 1)
            nc.vector.tensor_tensor(x2[:], ps[0:N, 6, 0:D], x1b[:], ALU.add).then_inc(ready("x2"), 1)
            dve.wait_ge(ready("x2"), 1)
            layernorm_dve(dve, "ln3", x2[:])
            dve.wait_ge(ready("ln3_hT_mm"), 1)
            nc.vector.tensor_copy(hT[:], ps[:, 5, 0:DC * N].rearrange("p (c n) -> p c n", c=DC)).then_inc(
                ready("ln3_hT"), 1)
            r = ready("route")
            route = [0]

            def link(i):
                route[0] += 1
                i.then_inc(r, 1)
                dve.wait_ge(r, route[0])

            dve.wait_ge(ready("gate_scores"), 1)
            dve.wait_ge(ready("ids_in"), 16)
            link(nc.vector.tensor_tensor(g_sel[:], g_sc[:], gb_sb[:], ALU.add))
            link(nc.vector.max(g_top[:], g_sel[:]))
            link(nc.vector.max_index(g_idx[:], g_top[:], g_sel[:]))
            link(nc.vector.tensor_copy(g_idf[:], g_idx[:]))
            link(nc.vector.tensor_scalar(g_m1[:], iota[:], g_idf[:, 0:1], None, ALU.is_equal))
            link(nc.vector.scalar_tensor_tensor(g_m[:], iota[:], g_idf[:, 1:2], g_m1[:], ALU.is_equal, ALU.add))
            link(nc.vector.tensor_tensor(g_w[:], g_m[:], g_sc[:], ALU.mult))
            link(nc.vector.tensor_reduce(g_sum[:, 0:1], g_w[:], AX_X, ALU.add))
            link(nc.vector.reciprocal(g_sum[:, 1:2], g_sum[:, 0:1]))
            link(nc.vector.tensor_scalar(g_we[:], g_w[:], g_sum[:, 1:2], None, ALU.mult))
            for g in range(E + 1):
                w = HS if g == 0 else H
                gate = ps[0:N, 1 if g == 0 else 2 + (g - 1) % 4, 0:w]
                up = ps[0:N, 0, 0:HS] if g == 0 else ps[0:N, 2 + (g - 1) % 4, H:2 * H]
                dve.wait_ge(sig_done, g + 1)
                nc.vector.tensor_tensor(act_g[:, g % 2, 0:w], gate, sig[:, g % 2, 0:w], ALU.mult).then_inc(gs_done, 1)
                dve.wait_ge(gs_done, g + 1)
                if g == 0:
                    nc.vector.tensor_tensor(h_sh, up, act_g[:, 0], ALU.mult).then_inc(hid_done, 1)
                else:
                    nc.vector.scalar_tensor_tensor(h_ex[:, g - 1], up, g_we[:, g - 1:g], act_g[:, g % 2, 0:w],
                                                   ALU.mult, ALU.mult).then_inc(hid_done, 1)
            dve.wait_ge(hT_mm, 1)
            nc.vector.tensor_copy(hsT[:, 0:2], ps[:, 0, 0:2 * N].rearrange("p (c n) -> p c n", n=N)).then_inc(
                ready("hsT"), 1)
            nc.vector.tensor_copy(hsT[0:HS - 2 * P, 2], ps[0:HS - 2 * P, 0, 2 * N:3 * N]).then_inc(ready("hsT"), 1)
            for b in range(2):
                dve.wait_ge(hT_mm, b + 2)
                nc.vector.tensor_copy(heT[:, b * E:(b + 1) * E], ps[0:HC, 6 + b].rearrange(
                    "p (c n) -> p c n", n=N)).then_inc(ready("heT"), 1)
            dve.wait_ge(ready("down_mm"), 1)
            nc.vector.tensor_tensor(x1[:], ps[0:N, 1, 0:D], x2[:], ALU.add).then_inc(ready("y"), 1)

        @block.tensor
        def _(pe):
            def transpose_h(name):
                pe.wait_ge(ready(name + "_h"), 1)
                for c in range(DC):
                    last = nc.tensor.transpose(ps[:, 5, c * N:(c + 1) * N], h_sb[:, c * P:(c + 1) * P],
                                               ident[0:N, 0:N])
                last.then_inc(ready(name + "_hT_mm"), 1)
                pe.wait_ge(ready(name + "_hT"), 1)

            def contract(dst, rhs, **flags):
                for c in range(DC):
                    last = nc.tensor.matmul(dst, hT[:, c, :], rhs(c), start=(c == 0), stop=(c == DC - 1))
                return last

            pe.wait_ge(ready("eye_in"), 16)
            transpose_h("ln1")
            pe.wait_ge(ready("wq_in"), 16)
            contract(ps[0:N, 4, 0:D], lambda c: wq_sb[:, c, :]).then_inc(ready("q_mm"), 1)
            pe.wait_ge(ready("zeros"), 1)
            for b in range(2):
                nc.tensor.matmul(ps[:, 6 + b, 0:PAIRS // 2 * VW], zeros[:, 0:P], zeros[:],
                                 start=True, stop=True, skip_group_check=True)
            pe.wait_ge(ready("ident16"), 1)
            pe.wait_ge(ready("q_parts"), 4)
            for c in range(KC):
                last = nc.tensor.transpose(
                    ps[:, 5, :].bitcast(F16)[:, c * N:(c + 1) * N],
                    q_parts[:, c * HPC:(c + 1) * HPC].rearrange("p h a d -> p (h a d)"), ident16[0:N, 0:N])
            last.then_inc(ready("qT_mm"), 1)
            pe.wait_ge(ready("q_blk"), HPC)
            pe.wait_ge(ready("wkv_lo"), 1)
            pe.wait_ge(ready("v_ones"), 1)

            def scores(t, half):
                if half == 0:
                    wait(pe, kT_copied, t.count(plus=1))
                wait(pe, exp_done, t.count(2, half - 1))
                for c in range(KC // 2):
                    last = nc.tensor.matmul(
                        ps_scores[half][:, c // 2, c % 2 * HPC * N:(c % 2 + 1) * HPC * N],
                        kT[:, t.slot(2), half * KC // 2 + c], q_blk[:, half * KC // 2 + c].rearrange(
                            "p h n -> p (h n)"), start=True, stop=True)
                last.then_inc(scores_mm, 1)

            def values(t, half):
                wait(pe, lo_done, t.count(2, half + 1))
                if half == 1:
                    wait(pe, low_pooled, t.count(plus=1))
                if half == 0:
                    wait(pe, v_done, t.count(plus=1))
                hi = probs[:, t.slot(2), half].bitcast(BF16)[:, 1::2]
                lo = probs_lo[:, t.slot(2), half]
                for r in range(PAIRS // 2):
                    for part in (hi, lo):
                        last = nc.tensor.matmul(ps_o[half][:, r], part[:, r * P:(r + 1) * P],
                                                v_sb[:, t.slot(4), half * PAIRS // 2 + r], start=False,
                                                stop=False, skip_group_check=True)
                last.then_inc(pv_done, 1)

            def step(t):
                pv, tr, kv = t.ahead(PV), t.ahead(TR), t.ahead(PROJ)
                for half in range(2):
                    if t.exists():
                        scores(t, half)
                    if pv.exists():
                        values(pv, half)
                if kv.exists():
                    wait(pe, ctx_lo_done, kv.count(plus=1))
                    wait(pe, kv_copied, kv.count())
                    a = kv.slot(2)
                    terms = [(lhs[:, a, c], rhs[:, c]) for c in range(DC)
                             for lhs, rhs in ((ctx_hi, wkv_hi), (ctx_hi, wkv_lo), (ctx_lo, wkv_hi))]
                    for n, (lhs, rhs) in enumerate(terms):
                        last = nc.tensor.matmul(ps_kv, lhs, rhs, start=(n == 0), stop=(n == len(terms) - 1))
                    last.then_inc(kv_mm, 1)
                if tr.exists():
                    wait(pe, k2_done, tr.count(plus=1))
                    wait(pe, kT_copied, tr.count())
                    for c in range(KC):
                        rows = k12[:, tr.slot(2), c * HPC:(c + 1) * HPC].rearrange("p h q a d -> p (h q a d)")
                        last = nc.tensor.transpose(ps_kT[:, c], rows, ident16[:])
                    last.then_inc(kT_mm, 1)

            steps(pe, step)

            transpose_h("ln2")
            for w in range(3):
                for n in range(w * NSL, (w + 1) * NSL):
                    if n >= 4:
                        pe.wait_ge(qkv_out, n - 3)
                    pe.wait_ge(deq_done, n + 1)
                    contract(ps[0:N, n % 4], lambda c: w_all[:, n, c * 512:(c + 1) * 512]).then_inc(qkv_mm, 1)
                if w:
                    bank = (4, 6)[w - 1]
                    pe.wait_ge(qkv_out, w * NSL)
                    for h in range(SH):
                        last = nc.tensor.transpose(ps[:, bank + h // 8, h % 8 * N:(h % 8 + 1) * N],
                                                   tok[:, w - 1, h * SD:(h + 1) * SD], ident[0:N, 0:N])
                    last.then_inc(ready(f"t{w}_mm"), 1)
            pe.wait_ge(ready("qkT"), 2)
            pe.wait_ge(qkv_out, NQKV)
            for h in range(SH):
                last = nc.tensor.matmul(ps[0:N, h // 8, h % 8 * N:(h % 8 + 1) * N], qT[:, h], kTs[:, h],
                                        start=True, stop=True)
            last.then_inc(ready("s_mm"), 1)
            pe.wait_ge(ready("s_p"), 1)
            for h in range(SH):
                last = nc.tensor.transpose(ps[0:N, 2 + h // 8, h % 8 * N:(h % 8 + 1) * N], s_p[:, h],
                                           ident[0:N, 0:N])
            last.then_inc(ready("pT_mm"), 1)
            pe.wait_ge(ready("pT"), 1)
            for h in range(SH):
                last = nc.tensor.matmul(ps[:, 4 + h // 8, h % 8 * N:(h % 8 + 1) * N],
                                        tok[:, 2, h * SD:(h + 1) * SD], pT[:, h], start=True, stop=True)
            last.then_inc(ready("oT_mm"), 1)
            pe.wait_ge(ready("oT"), 1)
            pe.wait_ge(wo_deq_done, NSL)
            wo = w_all[:, NQKV:].rearrange("p s (h n) -> p (s h) n", n=D)
            for h in range(SH):
                last = nc.tensor.matmul(ps[0:N, 6, 0:D], qT[:, h], wo[:, h], start=(h == 0), stop=(h == SH - 1))
            last.then_inc(ready("wo_mm"), 1)

            pe.wait_ge(ready("tail_in"), 9 * 16)
            transpose_h("ln3")
            contract(ps[0:N, 6, 0:E], lambda c: gate_sb[:, c, :]).then_inc(ready("gate_mm"), 1)
            contract(ps[0:N, 0, 0:HS], lambda c: sgw_sb[:, c, 0:HS])
            contract(ps[0:N, 1, 0:HS], lambda c: sgw_sb[:, c, HS:2 * HS]).then_inc(up_mm, 1)
            for e in range(E):
                if e >= 4:
                    pe.wait_ge(hid_done, e - 2)
                contract(ps[0:N, 2 + e % 4, 0:2 * H], lambda c: up_sb[:, c, e, :]).then_inc(up_mm, 1)
            pe.wait_ge(hid_done, 1)
            for c in range(3):
                w = min(P, HS - c * P)
                last = nc.tensor.transpose(ps[0:w, 0, c * N:(c + 1) * N], h_sh[:, c * P:c * P + w],
                                           ident[0:N, 0:N])
            last.then_inc(hT_mm, 1)
            pe.wait_ge(ready("gate_scores"), 1)
            for e in range(E):
                pe.wait_ge(hid_done, e + 2)
                for c in range(2):
                    k = 2 * e + c
                    last = nc.tensor.transpose(ps[0:HC, 6 + k // 8, k % 8 * N:(k % 8 + 1) * N],
                                               h_ex[:, e, c * HC:(c + 1) * HC], ident[0:N, 0:N])
                if e % 4 == 3:
                    last.then_inc(hT_mm, 1)
            pe.wait_ge(ready("hsT"), 2)
            for c in range(3):
                w = min(P, HS - c * P)
                nc.tensor.matmul(ps[0:N, 1, 0:D], hsT[0:w, c], sdw_sb[0:w, c], start=(c == 0), stop=False)
            for k in range(2 * E):
                if k % 8 == 0:
                    pe.wait_ge(ready("heT"), k // 8 + 1)
                last = nc.tensor.matmul(ps[0:N, 1, 0:D], heT[:, k], dn_sb[:, k // 2, k % 2], start=False,
                                        stop=(k == 2 * E - 1))
            last.then_inc(ready("down_mm"), 1)


def kernel(x, ctx_2048, L0_xattn_Wq, L0_xattn_Wk, L0_xattn_Wv, L0_attn_wq_codes, L0_attn_wq_scales,
           L0_attn_bq, L0_attn_wk_codes, L0_attn_wk_scales, L0_attn_bk, L0_attn_wv_codes,
           L0_attn_wv_scales, L0_attn_bv, L0_attn_wo_codes, L0_attn_wo_scales, L0_attn_bo,
           L0_ffn_gate_w, L0_ffn_gate_bias, L0_ffn_shared_gw, L0_ffn_shared_dw, L0_ffn_up_w,
           L0_ffn_down_w):
    import numpy as np
    import concourse.bacc as bacc
    from concourse.bass_utils import run_bass_kernel_spmd

    def rows(w):
        w = np.asarray(w)
        return w.reshape(DC, P, w.shape[1]).transpose(1, 0, 2)

    wkv = np.concatenate([np.asarray(L0_xattn_Wk), np.asarray(L0_xattn_Wv)])
    wkv = wkv.reshape(XH, XD, 2, D).transpose(2, 0, 1, 3).reshape(2 * D, D)
    codes = [rows(c).reshape(P, DC, NSL, 512).transpose(0, 2, 1, 3).reshape(P, NSL, WS) for c in (L0_attn_wq_codes, L0_attn_wk_codes, L0_attn_wv_codes)]
    codes.append(np.asarray(L0_attn_wo_codes).reshape(SH, SD, D).transpose(1, 0, 2).reshape(P, NSL, WS))
    nb = P // QB
    scales = [np.asarray(c).reshape(DC, nb, NSL, 512).transpose(2, 1, 0, 3).reshape(NSL, nb, WS)
              for c in (L0_attn_wq_scales, L0_attn_wk_scales, L0_attn_wv_scales)]
    scales.append(np.asarray(L0_attn_wo_scales).reshape(NSL, WS // D, nb, D).transpose(0, 2, 1, 3)
                  .reshape(NSL, nb, WS))
    up = np.asarray(L0_ffn_up_w).reshape(E * 2 * H, D).T
    arrays = {
        "x": np.asarray(x).reshape(N, D),
        "ctx_t": np.asarray(ctx_2048).reshape(T, P, DC, P).transpose(0, 3, 2, 1),
        "xwq": rows(np.asarray(L0_xattn_Wq).T),
        "xwkv": rows(wkv.T),
        "codes": np.concatenate(codes, axis=1),
        "scales": np.concatenate(scales),
        "qkv_bias": np.stack([np.asarray(b).reshape(SH, SD) for b in (L0_attn_bq, L0_attn_bk, L0_attn_bv)])
        .transpose(2, 0, 1),
        "bo": np.asarray(L0_attn_bo).reshape(1, D),
        "gate_w": rows(np.asarray(L0_ffn_gate_w).T),
        "gate_bias": np.asarray(L0_ffn_gate_bias).reshape(1, E),
        "shared_gw": rows(np.asarray(L0_ffn_shared_gw).T),
        "shared_dw": np.asarray(L0_ffn_shared_dw).T,
        "up_w": rows(up).reshape(P, DC, E, 2 * H),
        "down_w": np.asarray(L0_ffn_down_w).transpose(2, 0, 1).reshape(2, HC, E, D).transpose(1, 2, 0, 3),
        "eye": np.eye(P, dtype=np.float32),
        "expert_ids": np.tile(np.arange(E, dtype=np.float32), (N, 1)),
    }
    arrays = {n: np.ascontiguousarray(a) for n, a in arrays.items()}
    nc = bacc.Bacc("TRN2", target_bir_lowering=False, num_devices=1)
    args = [nc.dram_tensor(n, a.shape, mybir.dt.from_np(a.dtype), kind="ExternalInput").ap()
            for n, a in arrays.items()]
    out = nc.dram_tensor("out", (N, D), F32, kind="ExternalOutput").ap()
    perceiver(nc, *args, out)
    result = run_bass_kernel_spmd(nc, [arrays], core_ids=[0])
    return result.results[0]["out"].reshape(1, N, D)
```

```python
from contextlib import ExitStack

import concourse.bass as bass
from concourse import mybir

F32 = mybir.dt.float32
F32R = mybir.dt.float32r
F16 = mybir.dt.float16
BF16 = mybir.dt.bfloat16
U32 = mybir.dt.uint32
ACT = mybir.ActivationFunctionType
ALU = mybir.AluOpType
AX_X = mybir.AxisListType.X

P = 128
N = 64
D = 256
DC = D // P
M = 6272
T = M // P
XH, XD = 32, 8
PAIRS = XH // 2
TERMS = 3
ROWS = TERMS * XD
KC = XH * ROWS // P
HPC = 6
VW = 4 * XD + 1
HALF = N * XH // 2
SH, SD = 16, 128
GH = 4
G = SH // GH
FEAT = SH * SD
QB = 32
WS = 1024
POOLED = 640
SLOTS = 7
NSL = DC * FEAT // WS
NQKV = 3 * NSL
E, TOPK, H, HS = 8, 2, 176, 352
HC = H // 2
U = 4
PROJ, KV, TR, PV = 4, 3, 2, -1
FIRST, LAST = -(PROJ + 1), T - PV
LOOP0 = 1 - PV
ITERS = (T - PROJ - 1 - LOOP0) // U
LOOP1 = LOOP0 + ITERS * U
LN_EPS, RMS_EPS = 1e-5, 1e-6


class Tile:

    def __init__(self, i, c):
        self.i, self.c = i, c

    def ahead(self, k):
        return Tile(self.i, self.c + k)

    def exists(self):
        return self.i is not None or 0 <= self.c < T

    def slot(self, n):
        return self.c % n

    def count(self, per=1, plus=0):
        at = per * self.c + plus
        if self.i is None:
            return at if at > 0 else None
        return self.i * (U * per) + at

    def number(self):
        return self.c if self.i is None else self.i * U + self.c


def steps(engine, body, after):
    for c in range(FIRST, LOOP0):
        body(Tile(None, c))
        if c in after:
            after[c]()
    with engine.Fori(0, ITERS) as i:
        for j in range(U):
            body(Tile(i, LOOP0 + j))
    for c in range(LOOP1, LAST + 1):
        body(Tile(None, c))


def wait(engine, semaphore, count):
    if count is not None:
        engine.wait_ge(semaphore, count)


def perceiver(nc, x, ctx_t, xwq, xwkv, codes, scales, qkv_bias, bo, gate_w, gate_bias,
              shared_gw, shared_dw, up_w, down_w, eye, expert_ids, chunk_heads, out):
    with ExitStack() as stack:
        def sb(name, shape, dt=F32):
            return stack.enter_context(nc.sbuf_tensor(name, shape, dt))

        def sem(name):
            return stack.enter_context(nc.semaphore(name))

        once = {}

        def ready(name):
            if name not in once:
                once[name] = sem(name)
            return once[name]

        ident = sb("ident", [P, P])
        ident16 = sb("ident16", [P, P], F16)
        iota = sb("iota", [N, E])
        eps_ln = sb("eps_ln", [P, 1])
        eps_rms = sb("eps_rms", [P, 1])
        x_sb = sb("x_sb", [N, D])
        wq_sb = sb("wq_sb", [P, DC, D])
        wkv_f = sb("wkv_f", [P, DC, 2 * D])
        wkv_hi = sb("wkv_hi", [P, DC, 2 * D], F32R)
        wkv_lo = sb("wkv_lo", [P, DC, 2 * D], F32R)
        w_all = sb("w_all", [P, 4 * NSL, WS])
        s_ring = sb("s_ring", [P, 2, WS])
        bias_t = sb("bias_t", [SD, 3, SH])
        bo_sb = sb("bo_sb", [N, D])
        gate_sb = sb("gate_sb", [P, DC, E])
        gb_sb = sb("gb_sb", [N, E])
        sgw_sb = sb("sgw_sb", [P, DC, 2 * HS])
        sdw_sb = sb("sdw_sb", [P, 3, D])
        up_sb = sb("up_sb", [P, DC, E, 2 * H])
        dn_sb = sb("dn_sb", [HC, E, 2, D])
        ctx_f = sb("ctx_f", [P, 4, DC, P])
        ctx_hi = sb("ctx_hi", [P, 2, DC, P], F32R)
        ctx_lo = sb("ctx_lo", [P, 2, DC, P], F32R)
        kv_sb = sb("kv_sb", [P, 2, 2 * D])
        k_sq = sb("k_sq", [P, 2, D])
        k_ss = sb("k_ss", [P, 2, XH])
        k_ln = sb("k_ln", [P, 2, XH])
        k_r = sb("k_r", [P, 2, XH])
        k_n = sb("k_n", [P, 2, D])
        k12_room = sb("k12_room", [P, max(2 * WS, 2 * XH * ROWS)], F16)
        k12 = k12_room[:, 0:2 * XH * ROWS].rearrange("p (s h a d) -> p s h a d", s=2, h=XH, a=TERMS)
        v_flat = sb("v_flat", [P, 4 * PAIRS * VW], F16)
        v_sb = v_flat[:].rearrange("p (s r v) -> p s r v", s=4, r=PAIRS)
        kT_room = sb("kT_room", [P, max(2 * WS, 2 * KC * P)], F16)
        kT = kT_room[:, 0:2 * KC * P].rearrange("p (s c m) -> p s c m", s=2, c=KC)
        q_blk = sb("q_blk", [P, KC, HPC, N], F16)
        blk_mask = sb("blk_mask", [P, KC, HPC])
        zeros = sb("zeros", [P, PAIRS // 2 * VW], F16)
        room = sb("room", [P, 4 * HALF + 2 * HALF])
        probs = room[:, 0:4 * HALF].rearrange("p (s h n) -> p s h n", s=2, h=2)
        probs_lo = room[:, 4 * HALF:].bitcast(F16).rearrange("p (s h n) -> p s h n", s=2, h=2)
        tok_v = room[0:N, 0:FEAT]
        h_sb = sb("h_sb", [N, D])
        hT = sb("hT", [P, DC, N])
        bn = sb("bn", [N, 6])
        mv = sb("mv", [N, 2])
        rs = sb("rs", [N, 4])
        q_f = sb("q_f", [N, D])
        q_sq = sb("q_sq", [N, D])
        q_ss = sb("q_ss", [N, 3, XH])
        q_n = sb("q_n", [N, D])
        q_parts = sb("q_parts", [N, XH, TERMS, XD], F16)
        o_sb = sb("o_sb", [P, PAIRS, VW])
        o_sum = sb("o_sum", [P, PAIRS, 2 * XD])
        o_nrm = o_sum
        o_den = sb("o_den", [P, PAIRS])
        o_cat = sb("o_cat", [N, PAIRS, 2, XD])
        x1 = sb("x1", [N, D])
        x1b, x2 = q_f, q_sq
        qT = wkv_f[:].rearrange("p c (h n) -> p (c h) n", n=N)
        oT = wq_sb[:].rearrange("p c (h n) -> p (c h) n", n=N)
        s_slots = [s_ring[:, 0], s_ring[:, 1],
                   v_flat[:, 0:2 * WS].bitcast(F32)]
        s_slots += [room[:, FEAT + k * WS:FEAT + (k + 1) * WS] for k in range(SLOTS - 3)]
        wo_s_slots = [k12_room[:, 0:2 * WS].bitcast(F32), kT_room[:, 0:2 * WS].bitcast(F32)]
        kTs = ctx_f[:].rearrange("p s c (h n) -> p (s c h) n", n=N)
        s_p = kv_sb[0:N].rearrange("p s (h n) -> p (s h) n", n=N)
        pT = q_blk[0:N].rearrange("p c h n -> p (c h n)").bitcast(F32).rearrange(
            "p (h n) -> p h n", n=N)[:, 0:SH]
        s_max = sb("s_max", [N, SH])
        s_sum = sb("s_sum", [N, SH])
        s_inv = sb("s_inv", [N, SH])
        g_sc = sb("g_sc", [N, E])
        g_sel = sb("g_sel", [N, E])
        g_top = sb("g_top", [N, E])
        g_idx = sb("g_idx", [N, E], U32)
        g_idf = sb("g_idf", [N, E])
        g_m1 = sb("g_m1", [N, E])
        g_m = sb("g_m", [N, E])
        g_w = sb("g_w", [N, E])
        g_sum = sb("g_sum", [N, 2])
        g_we = sb("g_we", [N, E])
        cuts = [0]
        for size in (2 * HS, 2 * HS, HS, E * H, 2 * E * N, 3 * N):
            cuts.append(cuts[-1] + size)
        sig, act_g, h_sh, h_ex, heT, hsT = (room[:, a:b] for a, b in zip(cuts, cuts[1:]))
        sig = sig[0:N].rearrange("p (s n) -> p s n", s=2)
        act_g = act_g[0:N].rearrange("p (s n) -> p s n", s=2)
        h_sh = h_sh[0:N]
        h_ex = h_ex[0:N].rearrange("p (e n) -> p e n", e=E)
        heT = heT[0:HC].rearrange("p (k n) -> p k n", n=N)
        hsT = hsT.rearrange("p (c n) -> p c n", n=N)

        ps = stack.enter_context(nc.psum_tensor("ps", [P, 8, 512], F32))
        ps_scores = [ps[:, 0:2, :], ps[:, 2:4, :]]
        ps_kv = ps[:, 4, :]
        ps_kT = ps[:, 5, :].bitcast(F16)[:, 0:KC * P].rearrange("p (c m) -> p c m", c=KC)
        ps_o = [ps[:, 6 + b, 0:PAIRS // 2 * VW].rearrange("p (r v) -> p r v", v=VW) for b in range(2)]

        ctx_in = [sem(f"ctx_in{k}") for k in range(4)]
        ctx_hi_done, ctx_lo_done = sem("ctx_hi_done"), sem("ctx_lo_done")
        kv_mm, kv_copied, sq_done, ss_done = sem("kv_mm"), sem("kv_copied"), sem("sq_done"), sem("ss_done")
        ln_done, r_done, kn_done = sem("ln_done"), sem("r_done"), sem("kn_done")
        k1_done, k2_done, v1_done, v_done = sem("k1_done"), sem("k2_done"), sem("v1_done"), sem("v_done")
        kT_mm, kT_copied = sem("kT_mm"), sem("kT_copied")
        scores_mm, exp_done, lo_done, pv_done = sem("scores_mm"), sem("exp_done"), sem("lo_done"), sem("pv_done")
        low_pooled = sem("low_pooled")
        scales_in = [sem(f"scales_in{k}") for k in range(SLOTS)]
        wo_scales_in = [sem(f"wo_scales_in{k}") for k in range(2)]
        deq_done, wo_deq_done = sem("deq_done"), sem("wo_deq_done")
        qk_mm, v_mm, v_out = sem("qk_mm"), sem("v_mm"), sem("v_out")
        biased, att_mm, att_max, att_shifted = (
            sem("biased"), sem("att_mm"), sem("att_max"), sem("att_shifted"))
        att_exp, att_sum, att_inv, att_p, pT_mm, pT_out = (
            sem("att_exp"), sem("att_sum"), sem("att_inv"), sem("att_p"), sem("pT_mm"), sem("pT_out"))
        oT_mm, oT_out = sem("oT_mm"), sem("oT_out")
        up_mm, sig_done, gs_done, hid_done, hT_mm = (
            sem("up_mm"), sem("sig_done"), sem("gs_done"), sem("hid_done"), sem("hT_mm"))

        block = stack.enter_context(nc.Block())

        @block.sync
        def _(sp):
            sp.dma_start(x_sb[:], x).then_inc(ready("x_in"), 16)
            sp.dma_start(wkv_f[:], xwkv).then_inc(ready("wkv_in"), 16)

            def load(tile):
                wait(sp, ctx_hi_done, tile.count(plus=-3))
                wait(sp, ctx_lo_done, tile.count(plus=-3))
                sp.dma_start(ctx_f[:, tile.slot(4)], ctx_t[bass.ds(tile.number(), 1)].rearrange(
                    "t p c m -> p (t c) m")).then_inc(ctx_in[tile.slot(4)], 16)

            def load_codes(k, landed):
                sp.dma_start(w_all[:, bass.ds(k, 1)], codes[:, bass.ds(k, 1)]).then_inc(landed, 16)

            def load_scales(k, slot, landed):
                sp.dma_start(slot, scales[k].unsqueeze(1).to_broadcast([P // QB, QB, WS])).then_inc(landed, 16)

            ahead = U + LOOP0
            for t in range(2):
                load(Tile(None, t))
            sp.dma_start(wq_sb[:], xwq).then_inc(ready("wq_in"), 16)
            for t in range(2, ahead):
                load(Tile(None, t))
            turns = ITERS - 1
            assert turns <= NQKV
            with sp.Fori(0, turns) as i:
                for j in range(U):
                    load(Tile(i, ahead + j))
                load_codes(i, ready("codes_in"))
            for t in range(ahead + turns * U, T):
                load(Tile(None, t))
            for k in range(turns, NQKV):
                load_codes(k, ready("codes_in"))
            for n in range(2):
                load_scales(n, s_slots[n], scales_in[n])
            for k in range(NQKV, 4 * NSL):
                load_codes(k, ready("wo_codes_in"))
            for dst, src in ((bias_t[:], qkv_bias), (bo_sb[:], bo.to_broadcast([N, D])), (gate_sb[:], gate_w),
                             (gb_sb[:], gate_bias.to_broadcast([N, E])), (sgw_sb[:], shared_gw),
                             (sdw_sb[:, 0:2], shared_dw[0:2 * P].rearrange("(c p) n -> p c n", p=P)),
                             (sdw_sb[0:HS - 2 * P, 2], shared_dw[2 * P:HS]),
                             (up_sb[:], up_w), (dn_sb[:], down_w)):
                sp.dma_start(dst, src).then_inc(ready("tail_in"), 16)
            sp.wait_ge(pv_done, 2 * T)
            for n in range(2, NQKV):
                if n >= SLOTS:
                    sp.wait_ge(deq_done, n - SLOTS + 1)
                load_scales(n, s_slots[n % SLOTS], scales_in[n % SLOTS])
                if n % 3 == 2:
                    m = n // 3
                    if m >= 2:
                        sp.wait_ge(wo_deq_done, m - 1)
                    load_scales(NQKV + m, wo_s_slots[m % 2], wo_scales_in[m % 2])
            sp.wait_ge(ready("y"), 1)
            sp.dma_start(out, x1[:]).then_inc(ready("out_written"), 16)
            sp.wait_ge(ready("out_written"), 16)

        @block.gpsimd
        def _(pool):
            pool.memset(zeros[:], 0.0).then_inc(ready("zeros"), 1)
            pool.memset(v_sb[:, :, :, VW - 1], 1.0).then_inc(ready("v_ones"), 1)

            def step(t):
                split, keys, sq = t.ahead(PROJ + 1), t.ahead(TR), t.ahead(KV)
                if sq.exists():
                    wait(pool, kv_copied, sq.count(plus=1))
                    wait(pool, ss_done, sq.count(plus=-1))
                    nc.gpsimd.tensor_tensor(k_sq[:, sq.slot(2)], kv_sb[:, sq.slot(2), 0:D],
                                            kv_sb[:, sq.slot(2), 0:D], ALU.mult).then_inc(sq_done, 1)
                if keys.exists():
                    wait(pool, k1_done, keys.count(plus=1))
                    nc.gpsimd.tensor_tensor(
                        k12[:, keys.slot(2), :, 2, :],
                        k_n[:, keys.slot(2)].rearrange("p (h d) -> p h d", d=XD),
                        k12[:, keys.slot(2), :, 0, :], ALU.subtract).then_inc(k2_done, 1)
                if split.exists():
                    wait(pool, ctx_hi_done, split.count(plus=1))
                    nc.gpsimd.tensor_tensor(ctx_lo[:, split.slot(2)], ctx_f[:, split.slot(4)],
                                            ctx_hi[:, split.slot(2)].bitcast(F32),
                                            ALU.subtract).then_inc(ctx_lo_done, 1)
                if t.exists():
                    wait(pool, exp_done, t.count(2, 2))
                    wait(pool, pv_done, t.count(2, -2))
                    a = probs[:, t.slot(2), 1, HALF - POOLED:HALF]
                    nc.gpsimd.tensor_tensor(probs_lo[:, t.slot(2), 1, HALF - POOLED:HALF], a,
                                            a.bitcast(BF16)[:, 1::2], ALU.subtract).then_inc(low_pooled, 1)

            steps(pool, step, {})
            pool.wait_ge(ready("wo_codes_in"), NSL * 16)
            for m in range(NSL):
                pool.wait_ge(wo_scales_in[m % 2], (m // 2 + 1) * 16)
                w = w_all[:, NQKV + m]
                nc.gpsimd.tensor_tensor(w, w, wo_s_slots[m % 2], ALU.mult).then_inc(wo_deq_done, 1)

        def layernorm_act(act, name):
            act.wait_ge(ready(name + "_stats"), 2)
            nc.scalar.activation(rs[:, 0:1], mv[:, 1:2], ACT.Ln, bias=eps_ln[0:N]).then_inc(ready(name + "_ln"), 1)
            act.wait_ge(ready(name + "_ln"), 1)
            nc.scalar.activation(rs[:, 1:2], rs[:, 0:1], ACT.Exp, scale=-0.5).then_inc(ready(name + "_r"), 1)

        @block.scalar
        def _(act):
            nc.scalar.preload_act_table_set("natural_log_exp_and_others")
            act.dma_start(ident[:], eye).then_inc(ready("eye_in"), 16)
            act.dma_start(iota[:], expert_ids).then_inc(ready("ids_in"), 16)
            act.dma_start(blk_mask[:], chunk_heads).then_inc(ready("mask_in"), 16)
            act.wait_ge(ready("eps_set"), 2)
            layernorm_act(act, "ln1")

            def queries_copied():
                act.wait_ge(ready("q_mm"), 1)
                nc.scalar.activation(q_f[:], ps[0:N, 0, 0:D], ACT.Copy).then_inc(ready("q_copied"), 1)

            def queries_rms():
                act.wait_ge(ready("q_ss"), 1)
                nc.scalar.activation(q_ss[:, 1], q_ss[:, 0], ACT.Ln, bias=eps_rms[0:N],
                                     scale=1.0 / XD).then_inc(ready("q_ln"), 1)
                act.wait_ge(ready("q_ln"), 1)
                nc.scalar.activation(q_ss[:, 2], q_ss[:, 1], ACT.Exp, scale=-0.5).then_inc(ready("q_r"), 1)

            def exps(t, half):
                wait(act, scores_mm, t.count(2, half + 1))
                wait(act, pv_done, t.count(2, half - 3))
                nc.scalar.activation(probs[:, t.slot(2), half], ps_scores[half].rearrange("p b n -> p (b n)"),
                                     ACT.Exp).then_inc(exp_done, 1)

            def step(t):
                if t.exists():
                    exps(t, 0)
                if t.exists():
                    exps(t, 1)
                r = t.ahead(KV)
                if r.exists():
                    a = r.slot(2)
                    wait(act, ss_done, r.count(plus=1))
                    nc.scalar.activation(k_ln[:, a], k_ss[:, a], ACT.Ln, bias=eps_rms[:],
                                         scale=1.0 / XD).then_inc(ln_done, 1)
                    wait(act, ln_done, r.count(plus=1))
                    wait(act, kn_done, r.count(plus=-1))
                    nc.scalar.activation(k_r[:, a], k_ln[:, a], ACT.Exp, scale=-0.5).then_inc(r_done, 1)
                kv = t.ahead(PROJ)
                if kv.exists():
                    wait(act, kv_mm, kv.count(plus=1))
                    wait(act, sq_done, kv.count(plus=-1))
                    wait(act, v_done, kv.count(plus=-1))
                    wait(act, kn_done, kv.count(plus=-1))
                    nc.scalar.activation(kv_sb[:, kv.slot(2)], ps_kv, ACT.Copy).then_inc(kv_copied, 1)
                tr = t.ahead(TR)
                if tr.exists():
                    wait(act, kT_mm, tr.count(plus=1))
                    wait(act, scores_mm, tr.count(2, -2))
                    nc.scalar.activation(kT[:, tr.slot(2)], ps_kT, ACT.Copy).then_inc(kT_copied, 1)

            steps(act, step, {-4: queries_copied, -3: queries_rms})

            layernorm_act(act, "ln2")

            for g in range(G + 1):
                if g >= 1:
                    act.wait_ge(pT_mm, g)
                    nc.scalar.activation(pT[:, (g - 1) * GH:g * GH], ps[0:N, 5, 0:GH * N].rearrange(
                        "p (h n) -> p h n", n=N), ACT.Copy).then_inc(pT_out, 1)
                if g < G:
                    act.wait_ge(v_mm, g + 1)
                    nc.scalar.activation(tok_v[:, g * 512:(g + 1) * 512], ps[0:N, 2], ACT.Copy).then_inc(v_out, 1)
                    heads = slice(g * GH, (g + 1) * GH)
                    act.wait_ge(att_shifted, g + 1)
                    nc.scalar.activation(s_p[:, heads], s_p[:, heads], ACT.Exp,
                                         scale=float(SD) ** -0.5).then_inc(att_exp, 1)
            layernorm_act(act, "ln3")
            act.wait_ge(ready("gate_mm"), 1)
            nc.scalar.activation(g_sc[:], ps[0:N, 6, 0:E], ACT.Sigmoid).then_inc(ready("gate_scores"), 1)
            for g in range(E + 1):
                act.wait_ge(up_mm, g + 1)
                if g >= 2:
                    act.wait_ge(gs_done, g - 1)
                w = HS if g == 0 else H
                nc.scalar.activation(sig[:, g % 2, 0:w], ps[0:N, 1 if g == 0 else 2 + (g - 1) % 4, 0:w],
                                     ACT.Sigmoid).then_inc(sig_done, 1)

        def layernorm_dve(dve, name, src):
            st = ready(name + "_stats")
            nc.vector.bn_stats(bn[:], src).then_inc(st, 1)
            dve.wait_ge(st, 1)
            nc.vector.bn_aggr(mv[:], bn[:]).then_inc(st, 1)
            dve.wait_ge(st, 2)
            newton = ready(name + "_newton")
            nc.vector.tensor_scalar(rs[:, 2:3], mv[:, 1:2], LN_EPS, None, ALU.add).then_inc(newton, 1)
            dve.wait_ge(newton, 1)
            dve.wait_ge(ready(name + "_r"), 1)
            nc.vector.tensor_scalar(rs[:, 3:4], rs[:, 2:3], rs[:, 1:2], rs[:, 1:2], ALU.mult,
                                    ALU.mult).then_inc(newton, 1)
            dve.wait_ge(newton, 2)
            nc.vector.tensor_scalar(rs[:, 2:3], rs[:, 3:4], -0.5, 1.5, ALU.mult, ALU.add).then_inc(newton, 1)
            dve.wait_ge(newton, 3)
            nc.vector.tensor_scalar(rs[:, 3:4], rs[:, 2:3], rs[:, 1:2], None, ALU.mult).then_inc(newton, 1)
            dve.wait_ge(newton, 4)
            nc.vector.tensor_scalar(h_sb[:], src, mv[:, 0:1], rs[:, 3:4], ALU.subtract,
                                    ALU.mult).then_inc(ready(name + "_h"), 1)

        @block.vector
        def _(dve):
            nc.vector.memset(eps_ln[:], LN_EPS).then_inc(ready("eps_set"), 1)
            nc.vector.memset(eps_rms[:], RMS_EPS).then_inc(ready("eps_set"), 1)
            dve.wait_ge(ready("x_in"), 16)
            layernorm_dve(dve, "ln1", x_sb[:])
            dve.wait_ge(ready("eye_in"), 16)
            nc.vector.tensor_copy(ident16[:], ident[:]).then_inc(ready("ident16"), 1)
            dve.wait_ge(ready("wkv_in"), 16)
            nc.vector.tensor_copy(wkv_hi[:], wkv_f[:]).then_inc(ready("wkv_hi"), 1)
            dve.wait_ge(ready("wkv_hi"), 1)
            nc.vector.tensor_tensor(wkv_lo[:], wkv_f[:], wkv_hi[:].bitcast(F32), ALU.subtract).then_inc(
                ready("wkv_lo"), 1)
            dve.wait_ge(ready("ln1_hT_mm"), 1)
            nc.vector.tensor_copy(hT[:], ps[:, 5, 0:DC * N].rearrange("p (c n) -> p c n", c=DC)).then_inc(
                ready("ln1_hT"), 1)

            qn = q_n[:].rearrange("p (h d) -> p h d", d=XD)

            def queries_squared():
                dve.wait_ge(ready("q_copied"), 1)
                nc.vector.tensor_tensor(q_sq[:], q_f[:], q_f[:], ALU.mult).then_inc(ready("q_sq"), 1)
                dve.wait_ge(ready("q_sq"), 1)
                nc.vector.tensor_reduce(q_ss[:, 0], q_sq[:].rearrange("p (h d) -> p h d", d=XD), AX_X,
                                        ALU.add).then_inc(ready("q_ss"), 1)

            def queries_split():
                dve.wait_ge(ready("q_r"), 1)
                nc.vector.scalar_tensor_tensor(
                    qn, q_f[:].rearrange("p (h d) -> p h d", d=XD), float(XD) ** -0.5,
                    q_ss[:, 2].unsqueeze(2).to_broadcast([N, XH, XD]), ALU.mult, ALU.mult).then_inc(
                    ready("q_n"), 1)
                dve.wait_ge(ready("q_n"), 1)
                for a in (0, 2):
                    nc.vector.tensor_copy(q_parts[:, :, a, :], qn).then_inc(ready("q_parts"), 1)
                dve.wait_ge(ready("q_parts"), 2)
                nc.vector.tensor_tensor(q_parts[:, :, 1, :], qn, q_parts[:, :, 0, :],
                                        ALU.subtract).then_inc(ready("q_parts"), 1)

            def queries_placed():
                dve.wait_ge(ready("qT_mm"), 1)
                dve.wait_ge(ready("mask_in"), 16)
                q_t = ps[:, 1, :].bitcast(F16)[:, 0:KC * N].rearrange("p (c n) -> p c n", c=KC)
                nc.vector.tensor_tensor(q_blk[:], q_t.unsqueeze(2).to_broadcast([P, KC, HPC, N]),
                                        blk_mask[:].unsqueeze(3).to_broadcast([P, KC, HPC, N]),
                                        ALU.mult).then_inc(ready("q_blk"), 1)

            def low(t, half):
                w = HALF - half * POOLED
                a = probs[:, t.slot(2), half, 0:w]
                wait(dve, exp_done, t.count(2, half + 1))
                wait(dve, pv_done, t.count(2, half - 3))
                nc.vector.tensor_tensor(probs_lo[:, t.slot(2), half, 0:w], a, a.bitcast(BF16)[:, 1::2],
                                        ALU.subtract).then_inc(lo_done, 1)

            def step(t):
                split = t.ahead(PROJ + 1)
                if split.exists():
                    a = split.slot(4)
                    n = (split.c // 4 + 1) * 16
                    dve.wait_ge(ctx_in[a], n if split.i is None else split.i * (16 * U // 4) + n)
                    wait(dve, kv_mm, split.count(plus=-1))
                    nc.vector.tensor_copy(ctx_hi[:, split.slot(2)], ctx_f[:, a]).then_inc(ctx_hi_done, 1)
                r = t.ahead(KV)
                if r.exists():
                    wait(dve, sq_done, r.count(plus=1))
                    wait(dve, ln_done, r.count(plus=-1))
                    nc.vector.tensor_reduce(k_ss[:, r.slot(2)], k_sq[:, r.slot(2)].rearrange(
                        "p (h d) -> p h d", d=XD), AX_X, ALU.add).then_inc(ss_done, 1)
                if t.exists():
                    low(t, 0)
                if r.exists():
                    v = kv_sb[:, r.slot(2), D:2 * D].rearrange("p (r v) -> p r v", v=2 * XD)
                    hi, lo = v_sb[:, r.slot(4), :, 0:2 * XD], v_sb[:, r.slot(4), :, 2 * XD:4 * XD]
                    wait(dve, kv_copied, r.count(plus=1))
                    wait(dve, pv_done, r.count(2, -6))
                    nc.vector.tensor_copy(hi, v).then_inc(v1_done, 1)
                    wait(dve, v1_done, r.count(plus=1))
                    nc.vector.tensor_tensor(lo, v, hi, ALU.subtract).then_inc(v_done, 1)
                if t.exists():
                    low(t, 1)
                if r.exists():
                    kn = k_n[:, r.slot(2)].rearrange("p (h d) -> p h d", d=XD)
                    wait(dve, r_done, r.count(plus=1))
                    wait(dve, k2_done, r.count(plus=-1))
                    nc.vector.tensor_tensor(
                        kn, kv_sb[:, r.slot(2), 0:D].rearrange("p (h d) -> p h d", d=XD),
                        k_r[:, r.slot(2)].unsqueeze(2).to_broadcast([P, XH, XD]), ALU.mult).then_inc(kn_done, 1)
                    wait(dve, kn_done, r.count(plus=1))
                    wait(dve, kT_mm, r.count(plus=-1))
                    nc.vector.tensor_copy(k12[:, r.slot(2), :, 0:2, :], kn.unsqueeze(2).to_broadcast(
                        [P, XH, 2, XD])).then_inc(k1_done, 1)

            steps(dve, step, {-4: queries_squared, -3: queries_split, -2: queries_placed})

            dve.wait_ge(pv_done, 2 * T)
            for b in range(2):
                nc.vector.tensor_copy(o_sb[:, b * PAIRS // 2:(b + 1) * PAIRS // 2], ps_o[b]).then_inc(ready("o_sb"), 1)
            dve.wait_ge(ready("o_sb"), 2)
            nc.vector.tensor_tensor(o_sum[:], o_sb[:, :, 0:2 * XD], o_sb[:, :, 2 * XD:4 * XD], ALU.add).then_inc(
                ready("o_sum"), 1)
            nc.vector.reciprocal(o_den[:], o_sb[:, :, VW - 1]).then_inc(ready("o_sum"), 1)
            dve.wait_ge(ready("o_sum"), 2)
            nc.vector.tensor_tensor(o_nrm[:], o_sum[:], o_den[:].unsqueeze(2).to_broadcast([P, PAIRS, 2 * XD]),
                                    ALU.mult).then_inc(ready("o_nrm"), 1)
            dve.wait_ge(ready("o_nrm"), 1)
            for h in range(2):
                nc.vector.tensor_copy(o_cat[:, :, h, :], o_nrm[h * N:(h + 1) * N, :, h * XD:(h + 1) * XD]).then_inc(
                    ready("o_cat"), 1)
            dve.wait_ge(ready("o_cat"), 2)
            nc.vector.tensor_tensor(x1[:], x_sb[:], o_cat[:].rearrange("p r h d -> p (r h d)"), ALU.add).then_inc(
                ready("x1"), 1)
            dve.wait_ge(ready("x1"), 1)
            layernorm_dve(dve, "ln2", x1[:])
            dve.wait_ge(ready("tail_in"), 9 * 16)
            nc.vector.tensor_tensor(x1b[:], x1[:], bo_sb[:], ALU.add).then_inc(ready("x1b"), 1)
            dve.wait_ge(ready("ln2_hT_mm"), 1)
            nc.vector.tensor_copy(hT[:], ps[:, 5, 0:DC * N].rearrange("p (c n) -> p c n", c=DC)).then_inc(
                ready("ln2_hT"), 1)
            dve.wait_ge(ready("codes_in"), NQKV * 16)

            def dequantise(g, w):
                n = 3 * g + w
                dve.wait_ge(scales_in[n % SLOTS], (n // SLOTS + 1) * 16)
                nc.vector.tensor_tensor(w_all[:, n], w_all[:, n], s_slots[n % SLOTS], ALU.mult).then_inc(deq_done, 1)

            for w in range(3):
                dequantise(0, w)
            for g in range(G + 1):
                heads = slice(g * GH, (g + 1) * GH)
                if g < G:
                    dve.wait_ge(qk_mm, g + 1)
                    for w, dst in enumerate((qT, kTs)):
                        nc.vector.tensor_tensor(
                            dst[:, heads], ps[:, g % 2, w * GH * N:(w + 1) * GH * N].rearrange(
                                "p (h n) -> p h n", n=N),
                            bias_t[:, w, heads].unsqueeze(2).to_broadcast([SD, GH, N]), ALU.add).then_inc(
                            biased, 1)
                if g + 1 < G:
                    dequantise(g + 1, 0)
                if g >= 1:
                    dve.wait_ge(oT_mm, g)
                    nc.vector.tensor_tensor(
                        oT[:, (g - 1) % 2 * GH:(g - 1) % 2 * GH + GH],
                        ps[:, 6, 0:GH * N].rearrange("p (h n) -> p h n", n=N),
                        bias_t[:, 2, (g - 1) * GH:g * GH].unsqueeze(2).to_broadcast([SD, GH, N]),
                        ALU.add).then_inc(oT_out, 1)
                if g < G:
                    sc = ps[0:N, 4, 0:GH * N].rearrange("p (h n) -> p h n", n=N)
                    dve.wait_ge(att_mm, g + 1)
                    nc.vector.tensor_reduce(s_max[:, heads], sc, AX_X, ALU.max).then_inc(att_max, 1)
                    dve.wait_ge(att_max, g + 1)
                    nc.vector.tensor_tensor(s_p[:, heads], sc, s_max[:, heads].unsqueeze(2).to_broadcast(
                        [N, GH, N]), ALU.subtract).then_inc(att_shifted, 1)
                if g + 1 < G:
                    dequantise(g + 1, 1)
                if g < G:
                    dve.wait_ge(att_exp, g + 1)
                    nc.vector.tensor_reduce(s_sum[:, heads], s_p[:, heads], AX_X, ALU.add).then_inc(att_sum, 1)
                    dve.wait_ge(att_sum, g + 1)
                    nc.vector.reciprocal(s_inv[:, heads], s_sum[:, heads]).then_inc(att_inv, 1)
                    dve.wait_ge(att_inv, g + 1)
                    nc.vector.tensor_tensor(s_p[:, heads], s_p[:, heads], s_inv[:, heads].unsqueeze(2)
                                            .to_broadcast([N, GH, N]), ALU.mult).then_inc(att_p, 1)
                if g + 1 < G:
                    dequantise(g + 1, 2)
            dve.wait_ge(ready("wo_mm"), 1)
            dve.wait_ge(ready("x1b"), 1)
            nc.vector.tensor_tensor(x2[:], ps[0:N, 7, 0:D], x1b[:], ALU.add).then_inc(ready("x2"), 1)
            dve.wait_ge(ready("x2"), 1)
            layernorm_dve(dve, "ln3", x2[:])
            dve.wait_ge(ready("ln3_hT_mm"), 1)
            nc.vector.tensor_copy(hT[:], ps[:, 5, 0:DC * N].rearrange("p (c n) -> p c n", c=DC)).then_inc(
                ready("ln3_hT"), 1)
            r = ready("route")
            route = [0]

            def link(i):
                route[0] += 1
                i.then_inc(r, 1)
                dve.wait_ge(r, route[0])

            dve.wait_ge(ready("gate_scores"), 1)
            dve.wait_ge(ready("ids_in"), 16)
            link(nc.vector.tensor_tensor(g_sel[:], g_sc[:], gb_sb[:], ALU.add))
            link(nc.vector.max(g_top[:], g_sel[:]))
            link(nc.vector.max_index(g_idx[:], g_top[:], g_sel[:]))
            link(nc.vector.tensor_copy(g_idf[:], g_idx[:]))
            link(nc.vector.tensor_scalar(g_m1[:], iota[:], g_idf[:, 0:1], None, ALU.is_equal))
            link(nc.vector.scalar_tensor_tensor(g_m[:], iota[:], g_idf[:, 1:2], g_m1[:], ALU.is_equal, ALU.add))
            link(nc.vector.tensor_tensor(g_w[:], g_m[:], g_sc[:], ALU.mult))
            link(nc.vector.tensor_reduce(g_sum[:, 0:1], g_w[:], AX_X, ALU.add))
            link(nc.vector.reciprocal(g_sum[:, 1:2], g_sum[:, 0:1]))
            link(nc.vector.tensor_scalar(g_we[:], g_w[:], g_sum[:, 1:2], None, ALU.mult))
            for g in range(E + 1):
                w = HS if g == 0 else H
                gate = ps[0:N, 1 if g == 0 else 2 + (g - 1) % 4, 0:w]
                up = ps[0:N, 0, 0:HS] if g == 0 else ps[0:N, 2 + (g - 1) % 4, H:2 * H]
                dve.wait_ge(sig_done, g + 1)
                nc.vector.tensor_tensor(act_g[:, g % 2, 0:w], gate, sig[:, g % 2, 0:w], ALU.mult).then_inc(gs_done, 1)
                dve.wait_ge(gs_done, g + 1)
                if g == 0:
                    nc.vector.tensor_tensor(h_sh, up, act_g[:, 0], ALU.mult).then_inc(hid_done, 1)
                else:
                    nc.vector.scalar_tensor_tensor(h_ex[:, g - 1], up, g_we[:, g - 1:g], act_g[:, g % 2, 0:w],
                                                   ALU.mult, ALU.mult).then_inc(hid_done, 1)
            dve.wait_ge(hT_mm, 1)
            nc.vector.tensor_copy(hsT[:, 0:2], ps[:, 0, 0:2 * N].rearrange("p (c n) -> p c n", n=N)).then_inc(
                ready("hsT"), 1)
            nc.vector.tensor_copy(hsT[0:HS - 2 * P, 2], ps[0:HS - 2 * P, 0, 2 * N:3 * N]).then_inc(ready("hsT"), 1)
            for b in range(2):
                dve.wait_ge(hT_mm, b + 2)
                nc.vector.tensor_copy(heT[:, b * E:(b + 1) * E], ps[0:HC, 6 + b].rearrange(
                    "p (c n) -> p c n", n=N)).then_inc(ready("heT"), 1)
            dve.wait_ge(ready("down_mm"), 1)
            nc.vector.tensor_tensor(x1[:], ps[0:N, 1, 0:D], x2[:], ALU.add).then_inc(ready("y"), 1)

        @block.tensor
        def _(pe):
            def transpose_h(name):
                pe.wait_ge(ready(name + "_h"), 1)
                for c in range(DC):
                    last = nc.tensor.transpose(ps[:, 5, c * N:(c + 1) * N], h_sb[:, c * P:(c + 1) * P],
                                               ident[0:N, 0:N])
                last.then_inc(ready(name + "_hT_mm"), 1)
                pe.wait_ge(ready(name + "_hT"), 1)

            def contract(dst, rhs, **flags):
                for c in range(DC):
                    last = nc.tensor.matmul(dst, hT[:, c, :], rhs(c), start=(c == 0), stop=(c == DC - 1))
                return last

            pe.wait_ge(ready("eye_in"), 16)
            transpose_h("ln1")
            pe.wait_ge(ready("zeros"), 1)
            for b in range(2):
                nc.tensor.matmul(ps[:, 6 + b, 0:PAIRS // 2 * VW], zeros[:, 0:P], zeros[:],
                                 start=True, stop=True, skip_group_check=True)
            pe.wait_ge(ready("ident16"), 1)
            pe.wait_ge(ready("wkv_lo"), 1)

            def queries_mm():
                pe.wait_ge(ready("wq_in"), 16)
                contract(ps[0:N, 0, 0:D], lambda c: wq_sb[:, c, :]).then_inc(ready("q_mm"), 1)

            def queries_turned():
                pe.wait_ge(ready("q_parts"), 3)
                flat = q_parts[:].rearrange("p h a d -> p (h a d)")
                for c in range(KC):
                    last = nc.tensor.transpose(ps[:, 1, :].bitcast(F16)[:, c * N:(c + 1) * N],
                                               flat[:, c * P:(c + 1) * P], ident16[0:N, 0:N])
                last.then_inc(ready("qT_mm"), 1)
                pe.wait_ge(ready("q_blk"), 1)
                pe.wait_ge(ready("v_ones"), 1)

            def scores(t, half):
                if half == 0:
                    wait(pe, kT_copied, t.count(plus=1))
                wait(pe, exp_done, t.count(2, half - 1))
                for c in range(KC // 2):
                    k = half * KC // 2 + c
                    first = c * P // ROWS
                    for bank in range(2):
                        lo, hi = max(first, 8 * bank), min(first + HPC, 8 * bank + 8)
                        if lo >= hi:
                            continue
                        last = nc.tensor.matmul(
                            ps_scores[half][:, bank, (lo - 8 * bank) * N:(hi - 8 * bank) * N],
                            kT[:, t.slot(2), k], q_blk[:, k, lo - first:hi - first].rearrange("p h n -> p (h n)"),
                            start=(lo == 8 * bank), stop=(hi == 8 * bank + 8), skip_group_check=True)
                last.then_inc(scores_mm, 1)

            def values(t, half):
                wait(pe, lo_done, t.count(2, half + 1))
                if half == 1:
                    wait(pe, low_pooled, t.count(plus=1))
                if half == 0:
                    wait(pe, v_done, t.count(plus=1))
                hi = probs[:, t.slot(2), half].bitcast(BF16)[:, 1::2]
                lo = probs_lo[:, t.slot(2), half]
                for r in range(PAIRS // 2):
                    for part in (hi, lo):
                        last = nc.tensor.matmul(ps_o[half][:, r], part[:, r * P:(r + 1) * P],
                                                v_sb[:, t.slot(4), half * PAIRS // 2 + r], start=False,
                                                stop=False, skip_group_check=True)
                last.then_inc(pv_done, 1)

            def step(t):
                pv, tr, kv = t.ahead(PV), t.ahead(TR), t.ahead(PROJ)
                for half in range(2):
                    if t.exists():
                        scores(t, half)
                    if pv.exists():
                        values(pv, half)
                if kv.exists():
                    wait(pe, ctx_lo_done, kv.count(plus=1))
                    wait(pe, kv_copied, kv.count())
                    a = kv.slot(2)
                    terms = [(lhs[:, a, c], rhs[:, c]) for c in range(DC)
                             for lhs, rhs in ((ctx_hi, wkv_hi), (ctx_hi, wkv_lo), (ctx_lo, wkv_hi))]
                    for n, (lhs, rhs) in enumerate(terms):
                        last = nc.tensor.matmul(ps_kv, lhs, rhs, start=(n == 0), stop=(n == len(terms) - 1))
                    last.then_inc(kv_mm, 1)
                if tr.exists():
                    wait(pe, k2_done, tr.count(plus=1))
                    wait(pe, kT_copied, tr.count())
                    rows = k12[:, tr.slot(2)].rearrange("p h a d -> p (h a d)")
                    for c in range(KC):
                        last = nc.tensor.transpose(ps_kT[:, c], rows[:, c * P:(c + 1) * P], ident16[:])
                    last.then_inc(kT_mm, 1)

            steps(pe, step, {-4: queries_mm, -2: queries_turned})

            transpose_h("ln2")

            wo = w_all[:, NQKV:].rearrange("p s (h n) -> p (s h) n", n=D)
            for g in range(G + 1):
                if g < G:
                    if g >= 2:
                        pe.wait_ge(biased, 2 * (g - 1))
                    for w in range(2):
                        pe.wait_ge(deq_done, 3 * g + w + 1)
                        for h in range(GH):
                            for c in range(DC):
                                at = c * 512 + h * SD
                                last = nc.tensor.matmul(
                                    ps[:, g % 2, (w * GH + h) * N:(w * GH + h + 1) * N],
                                    w_all[:, 3 * g + w, at:at + SD], hT[:, c, :],
                                    start=(c == 0), stop=(c == DC - 1))
                    last.then_inc(qk_mm, 1)
                if g >= 1:
                    pe.wait_ge(att_p, g)
                    if g >= 2:
                        pe.wait_ge(pT_out, g - 1)
                    for h in range(GH):
                        last = nc.tensor.transpose(ps[0:N, 5, h * N:(h + 1) * N], s_p[:, (g - 1) * GH + h],
                                                   ident[0:N, 0:N])
                    last.then_inc(pT_mm, 1)
                if g < G:
                    if g >= 1:
                        pe.wait_ge(v_out, g)
                    pe.wait_ge(deq_done, 3 * g + 3)
                    contract(ps[0:N, 2], lambda c: w_all[:, 3 * g + 2, c * 512:(c + 1) * 512]).then_inc(v_mm, 1)
                if g >= 1:
                    pe.wait_ge(v_out, g)
                    pe.wait_ge(pT_out, g)
                    if g >= 2:
                        pe.wait_ge(oT_out, g - 1)
                    for h in range(GH):
                        k = (g - 1) * GH + h
                        last = nc.tensor.matmul(ps[:, 6, h * N:(h + 1) * N], tok_v[:, k * SD:(k + 1) * SD],
                                                pT[:, k], start=True, stop=True)
                    last.then_inc(oT_mm, 1)
                if g < G:
                    pe.wait_ge(biased, 2 * (g + 1))
                    if g >= 1:
                        pe.wait_ge(att_shifted, g)
                    for h in range(GH):
                        last = nc.tensor.matmul(ps[0:N, 4, h * N:(h + 1) * N], qT[:, g * GH + h],
                                                kTs[:, g * GH + h], start=True, stop=True)
                    last.then_inc(att_mm, 1)
                if g >= 1:
                    pe.wait_ge(wo_deq_done, g)
                    pe.wait_ge(oT_out, g)
                    for h in range(GH):
                        k = (g - 1) * GH + h
                        last = nc.tensor.matmul(ps[0:N, 7, 0:D], oT[:, (g - 1) % 2 * GH + h], wo[:, k],
                                                start=(k == 0), stop=(k == SH - 1))
            last.then_inc(ready("wo_mm"), 1)

            pe.wait_ge(ready("tail_in"), 9 * 16)
            transpose_h("ln3")
            contract(ps[0:N, 6, 0:E], lambda c: gate_sb[:, c, :]).then_inc(ready("gate_mm"), 1)
            contract(ps[0:N, 0, 0:HS], lambda c: sgw_sb[:, c, 0:HS])
            contract(ps[0:N, 1, 0:HS], lambda c: sgw_sb[:, c, HS:2 * HS]).then_inc(up_mm, 1)
            for e in range(E):
                if e >= 4:
                    pe.wait_ge(hid_done, e - 2)
                contract(ps[0:N, 2 + e % 4, 0:2 * H], lambda c: up_sb[:, c, e, :]).then_inc(up_mm, 1)
            pe.wait_ge(hid_done, 1)
            for c in range(3):
                w = min(P, HS - c * P)
                last = nc.tensor.transpose(ps[0:w, 0, c * N:(c + 1) * N], h_sh[:, c * P:c * P + w],
                                           ident[0:N, 0:N])
            last.then_inc(hT_mm, 1)
            pe.wait_ge(ready("gate_scores"), 1)
            for e in range(E):
                pe.wait_ge(hid_done, e + 2)
                for c in range(2):
                    k = 2 * e + c
                    last = nc.tensor.transpose(ps[0:HC, 6 + k // 8, k % 8 * N:(k % 8 + 1) * N],
                                               h_ex[:, e, c * HC:(c + 1) * HC], ident[0:N, 0:N])
                if e % 4 == 3:
                    last.then_inc(hT_mm, 1)
            pe.wait_ge(ready("hsT"), 2)
            for c in range(3):
                w = min(P, HS - c * P)
                nc.tensor.matmul(ps[0:N, 1, 0:D], hsT[0:w, c], sdw_sb[0:w, c], start=(c == 0), stop=False)
            for k in range(2 * E):
                if k % 8 == 0:
                    pe.wait_ge(ready("heT"), k // 8 + 1)
                last = nc.tensor.matmul(ps[0:N, 1, 0:D], heT[:, k], dn_sb[:, k // 2, k % 2], start=False,
                                        stop=(k == 2 * E - 1))
            last.then_inc(ready("down_mm"), 1)


def kernel(x, ctx_2048, L0_xattn_Wq, L0_xattn_Wk, L0_xattn_Wv, L0_attn_wq_codes, L0_attn_wq_scales,
           L0_attn_bq, L0_attn_wk_codes, L0_attn_wk_scales, L0_attn_bk, L0_attn_wv_codes,
           L0_attn_wv_scales, L0_attn_bv, L0_attn_wo_codes, L0_attn_wo_scales, L0_attn_bo,
           L0_ffn_gate_w, L0_ffn_gate_bias, L0_ffn_shared_gw, L0_ffn_shared_dw, L0_ffn_up_w,
           L0_ffn_down_w):
    import numpy as np
    import concourse.bacc as bacc
    from concourse.bass_utils import run_bass_kernel_spmd

    def rows(w):
        w = np.asarray(w)
        return w.reshape(DC, P, w.shape[1]).transpose(1, 0, 2)

    wkv = np.concatenate([np.asarray(L0_xattn_Wk), np.asarray(L0_xattn_Wv)])
    wkv = wkv.reshape(XH, XD, 2, D).transpose(2, 0, 1, 3).reshape(2 * D, D)
    codes = [rows(c).reshape(P, DC, NSL, 512).transpose(0, 2, 1, 3).reshape(P, NSL, WS) for c in (L0_attn_wq_codes, L0_attn_wk_codes, L0_attn_wv_codes)]
    codes = [np.stack(codes, axis=2).reshape(P, NQKV, WS)]
    codes.append(np.asarray(L0_attn_wo_codes).reshape(SH, SD, D).transpose(1, 0, 2).reshape(P, NSL, WS))
    nb = P // QB
    scales = [np.asarray(c).reshape(DC, nb, NSL, 512).transpose(2, 1, 0, 3).reshape(NSL, nb, WS)
              for c in (L0_attn_wq_scales, L0_attn_wk_scales, L0_attn_wv_scales)]
    scales = [np.stack(scales, axis=1).reshape(NQKV, nb, WS)]
    scales.append(np.asarray(L0_attn_wo_scales).reshape(NSL, WS // D, nb, D).transpose(0, 2, 1, 3)
                  .reshape(NSL, nb, WS))
    owner = np.arange(KC * P).reshape(KC, P) // ROWS
    mask = owner[:, :, None] == (np.arange(KC) * P // ROWS)[:, None, None] + np.arange(HPC)
    up = np.asarray(L0_ffn_up_w).reshape(E * 2 * H, D).T
    arrays = {
        "x": np.asarray(x).reshape(N, D),
        "ctx_t": np.asarray(ctx_2048).reshape(T, P, DC, P).transpose(0, 3, 2, 1),
        "xwq": rows(np.asarray(L0_xattn_Wq).T),
        "xwkv": rows(wkv.T),
        "codes": np.concatenate(codes, axis=1),
        "scales": np.concatenate(scales),
        "qkv_bias": np.stack([np.asarray(b).reshape(SH, SD) for b in (L0_attn_bq, L0_attn_bk, L0_attn_bv)])
        .transpose(2, 0, 1),
        "bo": np.asarray(L0_attn_bo).reshape(1, D),
        "gate_w": rows(np.asarray(L0_ffn_gate_w).T),
        "gate_bias": np.asarray(L0_ffn_gate_bias).reshape(1, E),
        "shared_gw": rows(np.asarray(L0_ffn_shared_gw).T),
        "shared_dw": np.asarray(L0_ffn_shared_dw).T,
        "up_w": rows(up).reshape(P, DC, E, 2 * H),
        "down_w": np.asarray(L0_ffn_down_w).transpose(2, 0, 1).reshape(2, HC, E, D).transpose(1, 2, 0, 3),
        "eye": np.eye(P, dtype=np.float32),
        "expert_ids": np.tile(np.arange(E, dtype=np.float32), (N, 1)),
        "chunk_heads": mask.transpose(1, 0, 2).astype(np.float32),
    }
    arrays = {n: np.ascontiguousarray(a) for n, a in arrays.items()}
    nc = bacc.Bacc("TRN2", target_bir_lowering=False, num_devices=1)
    args = [nc.dram_tensor(n, a.shape, mybir.dt.from_np(a.dtype), kind="ExternalInput").ap()
            for n, a in arrays.items()]
    out = nc.dram_tensor("out", (N, D), F32, kind="ExternalOutput").ap()
    perceiver(nc, *args, out)
    result = run_bass_kernel_spmd(nc, [arrays], core_ids=[0])
    return result.results[0]["out"].reshape(1, N, D)
```
